# Optimizing a Trainium2 kernel written in Bass

```python
import numpy as np
import jax
import jax.numpy as jnp

def _softmax(x, axis=-1):
    return jax.nn.softmax(x, axis=axis)

def _gelu(x):
    return jax.nn.gelu(x, approximate=True)

def _silu(x):
    return jax.nn.silu(x)

def _sigmoid(x):
    return jax.nn.sigmoid(x)

def _layernorm(x, axis=-1, eps=1e-05):
    m = jnp.mean(x, axis=axis, keepdims=True)
    v = jnp.var(x, axis=axis, keepdims=True)
    return (x - m) / jnp.sqrt(v + eps)

def _scatter_add(tgt, idx, src, axis=0):
    return tgt.at[idx].add(src)

def _segment_sum(src, seg, n):
    return jax.ops.segment_sum(src, seg, n)
kernel_name = 'mk_audio_tower_d1_tok_audfeat512_r4_3da636'

def setup_inputs(seed: int=0):
    np.random.seed(seed)
    _w = jnp.asarray

    def _rec_inputs():
        import jax
        import jax.numpy as jnp
        _rk = jax.random.key(seed)
        x = -0.000392918 + 0.999932 * jax.random.normal(jax.random.fold_in(_rk, 1), (64, 125, 128), jnp.float32)
        return x
    x = _rec_inputs()

    def _L0_tok_setup():
        import jax, jax.numpy as jnp
        import numpy as np
        from jax import lax
        B, T, D = (32, 256, 128)
        UNITS, WINDOW = (128, 3)
        key = jax.random.key(seed)
        k1, k2 = jax.random.split(key)
        x = jax.random.normal(k1, (B, T, D), dtype=jnp.float32)
        kernel = jax.random.normal(k2, (WINDOW, D, UNITS * 3), dtype=jnp.float32) * 0.05
        return {'x': x, 'kernel': kernel}
    _L0_tok_all = _L0_tok_setup()
    _L0_tok_in = {k: v for k, v in _L0_tok_all.items() if k in ('kernel',)}
    del _L0_tok_all

    def _L0_attn_setup():
        import jax, jax.numpy as jnp
        import numpy as np
        BATCH, SEQ, CH, ORDER = (4, 2048, 128, 64)

        def _rtf_kernel(A, B, L):
            C = A.shape[0]
            a = jnp.concatenate([jnp.ones((C, 1), A.dtype), A], axis=-1)
            a_f = jnp.fft.rfft(a, n=L, axis=-1)
            b_f = jnp.fft.rfft(B, n=L, axis=-1)
            return jnp.fft.irfft(b_f / a_f, n=L, axis=-1)
        key = jax.random.key(seed)
        k1, k2, k3 = jax.random.split(key, 3)
        x = jax.random.normal(k1, (BATCH, SEQ, CH), dtype=jnp.float32)
        A = 0.01 * jax.random.normal(k2, (CH, ORDER), dtype=jnp.float32)
        B = 0.01 * jax.random.normal(k3, (CH, ORDER), dtype=jnp.float32)
        h0 = jnp.zeros((1,), dtype=jnp.float32)
        return {'x': x, 'A': A, 'B': B, 'h0': h0}
    _L0_attn_all = _L0_attn_setup()
    _L0_attn_in = {k: v for k, v in _L0_attn_all.items() if k in ('A', 'B', 'h0')}
    del _L0_attn_all

    def _L0_ffn_setup():
        import jax, jax.numpy as jnp
        import numpy as np
        TOP_K = 2
        key = jax.random.key(seed)
        k1, k2, k3, k4 = jax.random.split(key, 4)
        B, S, D, F, E = (4, 128, 128, 512, 16)
        hidden_states = jax.random.normal(k1, (B, S, D), dtype=jnp.float32)
        gate_weight = jax.random.normal(k2, (E, D), dtype=jnp.float32) * 0.02
        w1 = jax.random.normal(k3, (E, F, D), dtype=jnp.float32) * 0.02
        w2 = jax.random.normal(k4, (E, D, F), dtype=jnp.float32) * 0.02
        return {'hidden_states': hidden_states, 'gate_weight': gate_weight, 'w1': w1, 'w2': w2}
    _L0_ffn_all = _L0_ffn_setup()
    _L0_ffn_in = {k: v for k, v in _L0_ffn_all.items() if k in ('gate_weight', 'w1', 'w2')}
    del _L0_ffn_all
    return {'x': x, 'L0_tok_kernel': _L0_tok_in['kernel'], 'L0_attn_A': _L0_attn_in['A'], 'L0_attn_B': _L0_attn_in['B'], 'L0_attn_h0': _L0_attn_in['h0'], 'L0_ffn_gate_weight': _L0_ffn_in['gate_weight'], 'L0_ffn_w1': _L0_ffn_in['w1'], 'L0_ffn_w2': _L0_ffn_in['w2']}

def reference(x, L0_tok_kernel, L0_attn_A, L0_attn_B, L0_attn_h0, L0_ffn_gate_weight, L0_ffn_w1, L0_ffn_w2):
    import jax
    import jax.numpy as jnp

    def _L0_tok_ref(x, kernel):
        import jax, jax.numpy as jnp
        import numpy as np
        from jax import lax
        B, T, D = (32, 256, 128)
        UNITS, WINDOW = (128, 3)
        units = kernel.shape[2] // 3
        conv = lax.conv_general_dilated(x, kernel, window_strides=(1,), padding='VALID', dimension_numbers=('NWC', 'WIO', 'NWC'))
        Z = conv[..., :units]
        F = conv[..., units:2 * units]
        O = conv[..., 2 * units:]
        z = jnp.tanh(Z)
        f = jax.nn.sigmoid(F)
        o = jax.nn.sigmoid(O)

        def step(c, zfo):
            z_t, f_t, o_t = zfo
            c_t = f_t * c + (1.0 - f_t) * z_t
            return (c_t, o_t * c_t)
        c0 = jnp.zeros((x.shape[0], units), dtype=x.dtype)
        zf = (z.transpose(1, 0, 2), f.transpose(1, 0, 2), o.transpose(1, 0, 2))
        _, hs = lax.scan(step, c0, zf)
        return hs.transpose(1, 0, 2)

    def _L0_attn_ref(x, A, B, h0):
        import jax, jax.numpy as jnp
        import numpy as np
        BATCH, SEQ, CH, ORDER = (4, 2048, 128, 64)

        def _rtf_kernel(A, B, L):
            C = A.shape[0]
            a = jnp.concatenate([jnp.ones((C, 1), A.dtype), A], axis=-1)
            a_f = jnp.fft.rfft(a, n=L, axis=-1)
            b_f = jnp.fft.rfft(B, n=L, axis=-1)
            return jnp.fft.irfft(b_f / a_f, n=L, axis=-1)
        Bt, L, C = x.shape
        K = _rtf_kernel(A, B, L)
        n_fft = 2 * L
        x_f = jnp.fft.rfft(x, n=n_fft, axis=1)
        k_f = jnp.fft.rfft(K, n=n_fft, axis=-1).T[None]
        h1 = jnp.fft.irfft(x_f * k_f, n=n_fft, axis=1)[:, :L]
        y1 = h1 + h0 * x
        return jax.nn.gelu(y1)

    def _L0_ffn_ref(hidden_states, gate_weight, w1, w2):
        import jax, jax.numpy as jnp
        import numpy as np
        TOP_K = 2
        B, S, D = hidden_states.shape
        E = gate_weight.shape[0]
        x = hidden_states.reshape(-1, D)
        gate_logits = x @ gate_weight.T
        top_vals, top_idx = jax.lax.top_k(gate_logits, TOP_K)
        routing_w = jax.nn.softmax(top_vals, axis=-1)
        mask = jnp.any(top_idx[:, :, None] == jnp.arange(E)[None, None, :], axis=1)
        h = jax.nn.silu(jnp.einsum('td,efd->tef', x, w1))
        counts = jnp.sum(mask, axis=0)
        h_sum = jnp.einsum('tef,te->ef', h, mask.astype(h.dtype))
        h_mean = h_sum / jnp.maximum(counts, 1)[:, None].astype(h.dtype)
        y_mean = jnp.einsum('ef,edf->ed', h_mean, w2)
        y_mean = jnp.where((counts > 0)[:, None], y_mean, 0.0)
        out = jnp.einsum('tk,tkd->td', routing_w, y_mean[top_idx])
        return out.reshape(B, S, D)
    h = _L0_tok_ref(x, L0_tok_kernel)
    h = h + _L0_attn_ref(_layernorm(h, axis=-1), L0_attn_A, L0_attn_B, L0_attn_h0)
    h = h + _L0_ffn_ref(_layernorm(h, axis=-1), L0_ffn_gate_weight, L0_ffn_w1, L0_ffn_w2)
    return h

_drawn_inputs = setup_inputs


def setup_inputs(seed=0):
    import zlib

    import numpy as np

    out = dict(_drawn_inputs(seed))
    spreads = {}
    factors = {'L0_attn_A': 5.213}
    for name, (base, spread) in spreads.items():
        noise = np.random.default_rng([zlib.crc32(name.encode()), seed]).standard_normal(out[name].shape)
        drawn = base * np.exp(spread * noise) if base else spread * noise
        out[name] = jnp.asarray(drawn.astype(out[name].dtype))
    for name, factor in factors.items():
        out[name] = (out[name] * factor).astype(out[name].dtype)
    return out
```

```python
from contextlib import ExitStack

import numpy as np

import concourse.bass as bass
from concourse import mybir

FP32 = mybir.dt.float32
BF16 = mybir.dt.bfloat16
I32 = mybir.dt.int32
ALU = mybir.AluOpType
ACT = mybir.ActivationFunctionType
AX = mybir.AxisListType

B, TIN, D = 64, 125, 128
WIN = 3
T = TIN - WIN + 1
ORDER = 64
NF = T // 2 + 1
E, FF = 16, 512
EPS = 1e-5

CB = 4
NCH = B // CB
CW = CB * T
XW = CB * TIN
XBUF = 4

CG = 8
NCG = D // CG
KROW = 256
HB = 8
NHB = B // HB

SLOT = 128
NTOK = B * T
NT = (2 * NTOK + E * (SLOT - 1)) // SLOT
GBUF = 6
assert NT % GBUF == 0 and NT <= 256
SPLIT = 112

EXPO = 32
NEG = -3.0e38
ARENA = 11128


def tables():
    n = np.arange(ORDER, dtype=np.float64)[:, None]
    k = np.arange(NF, dtype=np.float64)[None, :]
    w = 2 * np.pi * k / T
    m = np.arange(T, dtype=np.float64)[None, :]
    half = np.where(np.arange(NF) == 0, 1.0, 2.0)[:, None] / T
    ph = 2 * np.pi * k.T * m / T
    out = {
        "dft": np.concatenate([np.cos(w * n), -np.sin(w * n), np.cos(w * (n + 1)), -np.sin(w * (n + 1))], 1),
        "idft": np.concatenate([half * np.cos(ph), -half * np.sin(ph)], 1),
        "code": (1 + np.arange(128)[:, None] / 128.0) * 2.0 ** (np.arange(B)[None, :] - EXPO),
        "rank": np.tile(E - np.arange(E)[None, :], (128, 1)),
    }
    return {k: v.astype(np.float32) for k, v in out.items()}


def build(nc, x, wconv, fa, fb, h0, gate, w1, w2, dft, idft, code, rank, out, kpad, table):
    ctx = ExitStack()

    def sb(name, shape, dt=FP32):
        return ctx.enter_context(nc.sbuf_tensor(name, shape, dt))

    def pb(name):
        return ctx.enter_context(nc.psum_tensor(name, [128, 512], FP32))

    def sem(name):
        return ctx.enter_context(nc.semaphore(name))

    with ctx:
        BIG = sb("BIG", [128, 2 * E * FF])
        hank = BIG[:, 0:D * T].rearrange("p (c t) -> p c t", c=D)
        esum = BIG[:, 0:E * FF]
        w2_sb = BIG[:, E * FF:2 * E * FF].rearrange("p (e f) -> p e f", e=E)
        w1T = sb("w1T", [128, E * FF])
        H = sb("H", [128, B, D])
        XN = sb("XN", [128, B, D])
        arena = sb("arena", [128, ARENA])
        used = [0]

        def carve(*dims, dt=FP32):
            n = int(np.prod(dims))
            words = n if dt != BF16 else (n + 1) // 2
            part = arena[:, used[0]:used[0] + words]
            used[0] += words
            assert used[0] <= ARENA, used[0]
            if dt != FP32:
                part = part.bitcast(dt)[:, 0:n]
            if len(dims) == 2:
                part = part.rearrange("p (a b) -> p a b", a=dims[0])
            if len(dims) == 3:
                part = part.rearrange("p (a b c) -> p a b c", a=dims[0], b=dims[1])
            return part

        wk = carve(WIN, 3 * D)
        xin = carve(XBUF, CB, D)
        xT = carve(2, XW)
        w1in = carve(2, 4, D)
        zg = carve(2, CW)
        fg = carve(2, CW)
        og = carve(2, CW)
        cc = carve(2, CW)
        hT = carve(2, CW)
        hR = carve(2, CW)
        used[0] = 0
        gl = carve(2, CG, B)
        x2T = carve(2, 4, T)
        L = carve(B, E)
        LW = carve(B, E)
        OHS = carve(2, B, E)
        OH = [OHS[:, 0], OHS[:, 1]]
        cum = carve(E, B)
        tot = carve(E, B)
        G = carve(GBUF, D)
        maskb = carve(B * E, dt=BF16)
        ohl = carve(4, 128, dt=BF16)
        ohh = carve(4, NT + NT % 2, dt=BF16)
        posi = carve(3, 2 * B, dt=I32)
        hilo = carve(2, 2 * B)
        GT = carve(2, SLOT)
        st2 = carve(2, HB * 6).rearrange("p a (q n) -> p a q n", q=HB)
        small = carve(7, E)
        y = carve(2, E)
        S = OHS.rearrange("p a b e -> p (a b e)").rearrange("p (k f) -> p k f", k=4)
        RT = x2T.rearrange("p a b t -> p (a b) t")
        gl0 = gl[:, 0].rearrange("p c b -> p (c b)")
        gl1 = gl[:, 1].rearrange("p c b -> p (c b)")
        mx = gl0[:, 0:4 * B].rearrange("p (n b) -> p n b", n=4)
        pos = gl0[:, 4 * B:6 * B]
        wgt = gl1[:, 0:3 * B].rearrange("p (n b) -> p n b", n=3)
        idx = gl1[:, 3 * B:3 * B + NT].bitcast(I32)
        junk = gl0
        idx2 = GT.rearrange("p k s -> p (k s)")[:, 0:NT].bitcast(I32)
        lw = LW.rearrange("p b e -> p (b e)")
        eidf = lw[0:1, 0:2 * NT].rearrange("p (a n) -> p a n", a=2)
        eid = lw[0:1, 2 * NT:3 * NT].bitcast(I32)
        yT = lw[0:E, 3 * NT:3 * NT + D]
        ybd = cum.rearrange("p e b -> p (e b)").rearrange("p (b d) -> p b d", b=HB)

        st1 = sb("st1", [128, 2, CB, 6])
        mm1 = sb("mm1", [128, 2, 3, CB])
        ve1 = sb("ve1", [128, 2, CB])
        rs1 = sb("rs1", [128, 2, CB])
        mhalf = sb("mhalf", [128, HB])
        ident = sb("ident", [128, 128])
        fr = w1T[0:NF, 12 * FF:15 * FF].rearrange("p (a c) -> p a c", a=12)
        dft_sb = w1T[0:ORDER, 15 * FF:15 * FF + 4 * NF]
        idft_sb = w1T[0:NF, 15 * FF + 4 * NF:15 * FF + 4 * NF + 2 * T]
        ab = XN[:, B - 1].rearrange("p (a n) -> p a n", a=2)
        gate_in = XN[0:E, B - 4]
        kp = H[:, B - 2:B].rearrange("p a n -> p (a n)")
        abT = XN[0:ORDER, B - 3:B - 1]
        code_sb = sb("code_sb", [128, B])
        rank_sb = sb("rank_sb", [128, E])
        h0c = sb("h0c", [128, 1])
        gateT = sb("gateT", [128, E])
        mm2 = sb("mm2", [128, 2, 3, HB])
        ve2 = sb("ve2", [128, 2, HB])
        rs2 = sb("rs2", [128, 2, HB])
        trib = sb("trib", [128, 128], BF16)
        oneb = sb("oneb", [128, 128], BF16)
        smi = sb("smi", [128, 2, E], I32)
        iotb = sb("iotb", [128, NT], BF16)
        rep = sb("rep", [E, 128])
        bmask = sb("bmask", [128, HB])
        onef = sb("onef", [128, 128])

        P = [pb(f"P{n}") for n in range(8)]
        PG, PX, PH, PR, PW = P[0:3], P[3], P[4], P[5:7], P[7]

        const_in = sem("const_in")
        wk_in = sem("wk_in")
        ab_in = sem("ab_in")
        x_in = [sem(f"x_in{n}") for n in range(XBUF)]
        w1_in = [sem(f"w1_in{n}") for n in range(2)]
        w2_in = sem("w2_in")
        kpad_out = sem("kpad_out")
        hank_in = sem("hank_in")
        table_out = sem("table_out")
        zero_out = sem("zero_out")
        out_done = sem("out_done")
        pool_const = sem("pool_const")
        pool_step = sem("pool_step")
        ident_ok = sem("ident_ok")
        x_transposed = sem("x_transposed")
        xT_ready = sem("xT_ready")
        gate_mm = sem("gate_mm")
        gate_act = sem("gate_act")
        w1_transposed = sem("w1_transposed")
        w1T_ready = sem("w1T_ready")
        cell_step = sem("cell_step")
        h_ready = sem("h_ready")
        hR_ready = sem("hR_ready")
        h_transposed = sem("h_transposed")
        H_ready = sem("H_ready")
        bn1 = sem("bn1")
        ve1_ready = sem("ve1_ready")
        rstd1 = sem("rstd1")
        xn1_ready = sem("xn1_ready")
        filt_mm = sem("filt_mm")
        filt_ev = sem("filt_ev")
        filt_step = sem("filt_step")
        conv_mm = sem("conv_mm")
        gelu_done = sem("gelu_done")
        H_added = sem("H_added")
        bn2 = sem("bn2")
        ve2_ready = sem("ve2_ready")
        rstd2 = sem("rstd2")
        xn2_ready = sem("xn2_ready")
        x2_transposed = sem("x2_transposed")
        x2T_ready = sem("x2T_ready")
        logits_mm = sem("logits_mm")
        route_step = sem("route_step")
        mask_ready = sem("mask_ready")
        prefix_mm = sem("prefix_mm")
        diff_ready = sem("diff_ready")
        wgt_ready = sem("wgt_ready")
        onehot = sem("onehot")
        code_mm = sem("code_mm")
        idx_ready = sem("idx_ready")
        eid_ready = sem("eid_ready")
        esum_clear = sem("esum_clear")
        gathered = [sem(f"gathered{n}") for n in range(GBUF)]
        g_transposed = sem("g_transposed")
        GT_ready = sem("GT_ready")
        expert_mm = sem("expert_mm")
        silu_done = sem("silu_done")
        esum_step = sem("esum_step")
        hsum_mm = sem("hsum_mm")
        y_step = sem("y_step")
        R_ready = sem("R_ready")
        tail_mm = sem("tail_mm")
        tail_ev = sem("tail_ev")
        mix_mm = sem("mix_mm")
        mixed = sem("mixed")

        xr = x.rearrange("(n b) t d -> n t b d", b=CB)
        w1r = w1.rearrange("e (q p) d -> e p q d", p=128)
        FILT_EV, FILT_LAST = 4, 12

        block = ctx.enter_context(nc.Block())

        @block.sync
        def _(sp):
            sp.dma_start(xin[0:TIN, 0], xr[0]).then_inc(x_in[0], 16)
            sp.dma_start(wk[:], wconv.rearrange("w d n -> d w n")).then_inc(wk_in, 16)
            for n in range(1, XBUF):
                sp.dma_start(xin[0:TIN, n], xr[n]).then_inc(x_in[n], 16)
            sp.dma_start(ab[:, 0], fa).then_inc(ab_in, 16)
            sp.dma_start(ab[:, 1], fb).then_inc(ab_in, 16)
            sp.dma_start(dft_sb[:], dft).then_inc(ab_in, 16)
            sp.dma_start(idft_sb[:], idft).then_inc(ab_in, 16)
            sp.dma_start(h0c[:], bass.AP(h0.tensor, 0, [[0, 128], [1, 1]])).then_inc(ab_in, 16)
            sp.dma_start(gate_in[:], gate).then_inc(ab_in, 16)
            sp.dma_start(code_sb[:], code).then_inc(const_in, 16)
            sp.dma_start(rank_sb[:], rank).then_inc(const_in, 16)
            for n in range(2):
                sp.dma_start(w1in[:, n], w1r[n]).then_inc(w1_in[n], 16)
            for c in range(2, NCH):
                sp.wait_ge(w1_transposed, c - 1)
                sp.dma_start(w1in[:, c % 2], w1r[c]).then_inc(w1_in[c % 2], 16)
                if c + 2 < NCH and c + 2 >= XBUF:
                    sp.wait_ge(x_transposed, c + 3 - XBUF)
                    sp.dma_start(xin[0:TIN, (c + 2) % XBUF], xr[c + 2]).then_inc(x_in[(c + 2) % XBUF], 16)
                if c == 2:
                    sp.wait_ge(filt_step, FILT_LAST)
                    sp.dma_start(kpad, kp[:]).then_inc(kpad_out, 16)
                    sp.wait_ge(kpad_out, 16)
                    sp.dma_start(hank, bass.AP(kpad.tensor, 0, [[1, 128], [KROW, D], [1, T]])).then_inc(hank_in, 16)
            sp.wait_ge(conv_mm, NCG)
            sp.dma_start(w2_sb, w2.rearrange("e d f -> d e f")).then_inc(w2_in, 16)
            tv = table[1:, :].rearrange("(b t) d -> t b d", t=T)
            for g in range(NHB):
                sp.wait_ge(xn2_ready, g + 1)
                for lo, hi in ((0, SPLIT), (SPLIT, T)):
                    sp.dma_start(tv[lo:hi, g * HB:(g + 1) * HB], XN[lo:hi, g * HB:(g + 1) * HB]).then_inc(table_out, 16)
            sp.wait_ge(esum_clear, 1)
            sp.dma_start(table[0:1, :], esum[0:1, 0:D]).then_inc(zero_out, 16)
            ov = out.rearrange("b t d -> t b d")
            for g in range(NHB):
                sp.wait_ge(mixed, 2 * (g + 1))
                for lo, hi in ((0, SPLIT), (SPLIT, T)):
                    sp.dma_start(ov[lo:hi, g * HB:(g + 1) * HB], H[lo:hi, g * HB:(g + 1) * HB]).then_inc(out_done, 16)
            sp.wait_ge(out_done, 2 * NHB * 16)

        @block.gpsimd
        def _(pool):
            pool.memset(onef[:], 1.0)
            pool.memset(oneb[:], 1.0)
            pool.memset(mhalf[:], -0.5)
            pool.memset(kp[:], 0.0).then_inc(pool_const, 1)
            pool.wait_ge(pool_const, 1)
            pool.affine_select(out=ident[:], in_=onef[:], compare_op=ALU.is_equal, fill=0.0, base=0,
                               pattern=[[-1, 128]], channel_multiplier=1).then_inc(ident_ok, 1)
            pool.affine_select(out=trib[:], in_=onef[:], compare_op=ALU.is_gt, fill=0.0, base=0,
                               pattern=[[1, 128]], channel_multiplier=-1)
            pool.affine_select(out=rep[:].rearrange("p (b e) -> p b e", b=HB),
                               in_=onef[0:E, :].rearrange("p (b e) -> p b e", b=HB),
                               compare_op=ALU.is_equal, fill=0.0, base=0,
                               pattern=[[0, HB], [-1, E]], channel_multiplier=1)
            pool.affine_select(out=bmask[:], in_=onef[:, 0:HB], compare_op=ALU.is_ge, fill=0.0, base=0,
                               pattern=[[-E, HB]], channel_multiplier=1).then_inc(pool_step, 1)
            pool.wait_ge(pool_step, 1)
            pool.affine_select(out=bmask[:], in_=bmask[:], compare_op=ALU.is_gt, fill=0.0, base=E,
                               pattern=[[E, HB]], channel_multiplier=-1)
            pool.iota(iotb[:], pattern=[[1, NT]], base=0, channel_multiplier=0,
                      allow_small_or_imprecise_dtypes=True).then_inc(pool_const, 1)

            def reverse(c, k):
                pool.wait_ge(cell_step, 3 * c + 3)
                cv, ov, dst = (a[:, k].rearrange("p (b t) -> p b t", b=CB) for a in (cc, og, hR))
                nc.gpsimd.tensor_tensor(dst[:, :, ::-1], cv, ov, ALU.mult).then_inc(hR_ready, 1)

            def rstd(c, k):
                pool.wait_ge(ve1_ready, c + 1)
                nc.gpsimd.tensor_tensor(rs1[0:T, k], ve1[0:T, k], mhalf[0:T, 0:CB], ALU.pow).then_inc(rstd1, 1)

            for c in range(2):
                if c >= 1:
                    rstd(c - 1, (c - 1) % 2)
                reverse(c, c % 2)
            with pool.Fori(1, NCH // 2) as i:
                for k in range(2):
                    rstd(i * 2 + (k - 1), 1 - k)
                    pool.wait_ge(h_transposed, i * 2 + (k - 1))
                    reverse(i * 2 + k, k)
            rstd(NCH - 1, (NCH - 1) % 2)
            for g in range(NHB):
                pool.wait_ge(ve2_ready, g + 1)
                if g >= 2:
                    pool.wait_ge(xn2_ready, g - 1)
                nc.gpsimd.tensor_tensor(rs2[0:T, g % 2], ve2[0:T, g % 2], mhalf[0:T], ALU.pow).then_inc(rstd2, 1)
            pool.wait_ge(idx_ready, 1)
            pool.wait_ge(table_out, 2 * NHB * 16)
            pool.wait_ge(zero_out, 16)
            for n in range(NT):
                if n >= GBUF:
                    pool.wait_ge(g_transposed, n - GBUF + 1)
                pool.indirect_dma_start(
                    out=G[:, n % GBUF, :], out_offset=None, in_=table[:, :],
                    in_offset=bass.IndirectOffsetOnAxis(ap=idx[:, n:n + 1], axis=0),
                ).then_inc(gathered[n % GBUF], 16)

        @block.tensor
        def _(pe):
            def x_transposes(c, k, nth):
                pe.wait_ge(x_in[k], 16 * (nth + 1))
                if not (isinstance(c, int) and c == 0):
                    pe.wait_ge(xT_ready, c)
                for q in range(CB):
                    mm = nc.tensor.transpose(PX[:, q * TIN:(q + 1) * TIN], xin[0:TIN, k, q], ident[0:TIN, 0:TIN])
                mm.then_inc(x_transposed, 1)

            def gates(c, k, first):
                pe.wait_ge(xT_ready, c + 1)
                xv = xT[:, k].rearrange("p (b t) -> p b t", b=CB)
                for g in range(3):
                    if not first:
                        pe.wait_ge(gate_act, 3 * c - 3 + g + 1)
                    for w in range(WIN):
                        mm = nc.tensor.matmul(PG[g][:, 0:CW], wk[:, w, g * D:(g + 1) * D], xv[:, :, w:w + T],
                                              start=(w == 0), stop=(w == WIN - 1))
                    mm.then_inc(gate_mm, 1)

            def h_transposes(c, k, first, second):
                pe.wait_ge(h_ready, c + 1)
                pe.wait_ge(hR_ready, c + 1)
                if not first:
                    pe.wait_ge(H_ready, c)
                for q in range(CB):
                    nc.tensor.transpose(PH[0:T, q * D:(q + 1) * D], hT[:, k, q * T:(q + 1) * T], ident[:])
                if not (first or second):
                    pe.wait_ge(xn1_ready, c - 1)
                for q in range(CB):
                    mm = nc.tensor.transpose(PR[k][0:T, q * D:(q + 1) * D], hR[:, k, q * T:(q + 1) * T], ident[:])
                mm.then_inc(h_transposed, 1)

            def w1_transposes(e, k, nth, first):
                pe.wait_ge(w1_in[k], 16 * (nth + 1))
                if not first:
                    pe.wait_ge(w1T_ready, e)
                for q in range(4):
                    mm = nc.tensor.transpose(PW[:, q * 128:(q + 1) * 128], w1in[:, k, q], ident[:])
                mm.then_inc(w1_transposed, 1)

            def logits(n):
                pe.wait_ge(x2T_ready, n + 1)
                bank, at = P[n // 8], (n % 8) * 64
                for q in range(4):
                    mm = nc.tensor.matmul(bank[0:T, at + q * E:at + (q + 1) * E], x2T[:, n % 2, q], gateT[:],
                                          start=True, stop=True)
                mm.then_inc(logits_mm, 1)

            pe.wait_ge(ident_ok, 1)
            pe.wait_ge(pool_const, 2)
            x_transposes(0, 0, 0)
            pe.wait_ge(ab_in, 96)
            for n in range(2):
                nc.tensor.transpose(PW[0:ORDER, n * 128:(n + 1) * 128], ab[:, n], ident[:])
            mm = nc.tensor.transpose(PW[:, 256:256 + E], gate_in[:], ident[0:E, 0:E])
            mm.then_inc(filt_mm, 1)
            x_transposes(1, 1, 0)
            pe.wait_ge(wk_in, 16)
            gates(0, 0, True)
            pe.wait_ge(filt_ev, 1)
            for n, which in enumerate((1, 1, 0, 0)):
                mm = nc.tensor.matmul(PW[0:NF, n * 128:(n + 1) * 128], dft_sb[:, n * NF:(n + 1) * NF],
                                      abT[:, which], start=True, stop=True)
            mm.then_inc(filt_mm, 1)
            x_transposes(2, 2, 0)
            gates(1, 1, False)
            pe.wait_ge(filt_step, FILT_LAST - 1)
            nc.tensor.matmul(PW[:, 0:T], fr[:, 10], idft_sb[:, 0:T], start=True, stop=False)
            nc.tensor.matmul(PW[:, 0:T], fr[:, 11], idft_sb[:, T:2 * T], start=False, stop=True).then_inc(filt_mm, 1)
            h_transposes(0, 0, True, False)
            pe.wait_ge(filt_step, FILT_LAST)
            w1_transposes(0, 0, 0, True)
            for c in range(2, 4):
                x_transposes(c + 1, (c + 1) % XBUF, (c + 1) // XBUF)
                gates(c, c % 2, False)
                h_transposes(c - 1, (c - 1) % 2, False, c == 2)
                w1_transposes(c - 1, (c - 1) % 2, (c - 1) // 2, False)
            with pe.Fori(1, NCH // 4 - 1) as i:
                for k in range(4):
                    c = i * 4 + k
                    x_transposes(c + 1, (k + 1) % XBUF, i + (k + 1) // XBUF)
                    gates(c, k % 2, False)
                    h_transposes(c - 1, (k + 1) % 2, False, False)
                    w1_transposes(c - 1, (k + 1) % 2, i * 2 + (k + 1) // 2 - 1, False)
            for c in range(NCH - 4, NCH):
                if c + 1 < NCH:
                    x_transposes(c + 1, (c + 1) % XBUF, (c + 1) // XBUF)
                gates(c, c % 2, False)
                h_transposes(c - 1, (c - 1) % 2, False, False)
                w1_transposes(c - 1, (c - 1) % 2, (c - 1) // 2, False)
            h_transposes(NCH - 1, (NCH - 1) % 2, False, False)
            w1_transposes(NCH - 1, (NCH - 1) % 2, (NCH - 1) // 2, False)
            pe.wait_ge(hank_in, 16)
            pe.wait_ge(xn1_ready, NCH)
            for g in range(NCG):
                if g >= 3:
                    pe.wait_ge(gelu_done, g - 2)
                for j in range(CG):
                    c = g * CG + j
                    mm = nc.tensor.matmul(PG[g % 3][0:T, j * B:(j + 1) * B], hank[0:T, c, :], XN[0:T, :, c],
                                          start=True, stop=True)
                mm.then_inc(conv_mm, 1)

            for n in range(2 * NHB):
                pe.wait_ge(xn2_ready, n // 2 + 1)
                if n >= 2:
                    pe.wait_ge(x2T_ready, n - 1)
                for q in range(4):
                    mm = nc.tensor.transpose(PR[n % 2][:, q * T:(q + 1) * T], XN[0:T, 4 * n + q], ident[0:T, 0:T])
                mm.then_inc(x2_transposed, 1)
                if n >= 1:
                    logits(n - 1)
            logits(2 * NHB - 1)

            pe.wait_ge(mask_ready, 1)
            for h in range(2):
                nc.tensor.matmul(P[h][0:T, :], trib[0:T, 0:T], maskb[0:T, h * 512:(h + 1) * 512], start=True, stop=True)
            for h in range(2):
                mm = nc.tensor.matmul(P[2 + h][0:128, :], oneb[0:T, :], maskb[0:T, h * 512:(h + 1) * 512],
                                      start=True, stop=True)
            mm.then_inc(prefix_mm, 1)

            pe.wait_ge(onehot, 1)
            pe.wait_ge(route_step, 1)
            for n in range(2 * B):
                pe.wait_ge(onehot, n + 1)
                mm = nc.tensor.matmul(P[4][:, 0:NT], ohl[0:T, n % 4], ohh[0:T, n % 4, 0:NT], start=(n == 0), stop=(n == 2 * B - 1))
                mm.then_inc(code_mm, 1)

            pe.wait_ge(R_ready, 1)
            for g in range(NHB):
                if g >= 2:
                    pe.wait_ge(tail_ev, g - 1)
                mm = nc.tensor.transpose(P[6 + g % 2][:, 0:T], L[0:T, g * HB:(g + 1) * HB].rearrange("p b e -> p (b e)"),
                                         ident[0:T, 0:T])
                mm.then_inc(tail_mm, 1)

            def g_transpose(n, k, nth):
                pe.wait_ge(gathered[k], 16 * (nth + 1))
                if not (isinstance(n, int) and n < 2):
                    pe.wait_ge(GT_ready, n - 1)
                nc.tensor.transpose(P[4 + k % 2][:, 0:SLOT], G[:, k], ident[:]).then_inc(g_transposed, 1)

            def expert(n, k, first):
                e = pe.value_load(eid[0:1, bass.ds(n, 1)], min_val=0, max_val=E - 1)
                pe.wait_ge(GT_ready, n + 1)
                if not first:
                    pe.wait_ge(silu_done, n - 3)
                nc.tensor.matmul(P[k % 4][:, :], GT[:, k % 2], w1T[:, bass.ds(e * FF, FF)],
                                 start=True, stop=True).then_inc(expert_mm, 1)

            pe.wait_ge(idx_ready, 1)
            pe.wait_ge(tail_ev, NHB)
            pe.wait_ge(eid_ready, 1)
            for n in range(12):
                g_transpose(n, n % GBUF, n // GBUF)
                if n >= 1:
                    expert(n - 1, n - 1, n - 1 < 4)
            with pe.Fori(1, NT // 12) as i:
                for k in range(12):
                    g_transpose(i * 12 + k, k % GBUF, i * 2 + k // GBUF)
                    expert(i * 12 + (k - 1), (k - 1) % 12, False)
            for n in range(NT // 12 * 12, NT):
                g_transpose(n, n % GBUF, n // GBUF)
                expert(n - 1, (n - 1) % 12, False)
            expert(NT - 1, (NT - 1) % 12, False)

            pe.wait_ge(esum_step, NT)
            for e in range(E):
                if e >= 4:
                    pe.wait_ge(y_step, e - 3)
                nc.tensor.matmul(P[e % 4][:, :], onef[:], esum[:, e * FF:(e + 1) * FF],
                                 start=True, stop=True).then_inc(hsum_mm, 1)
            pe.wait_ge(y_step, E + 1)
            nc.tensor.transpose(P[4][0:E, 0:128], y[:, 1, :], ident[:]).then_inc(tail_mm, 1)
            pe.wait_ge(tail_ev, NHB + 1)
            nc.tensor.matmul(P[5][:, 0:128], rep[:], yT[:], start=True, stop=True).then_inc(tail_mm, 1)
            pe.wait_ge(tail_ev, NHB + 2)
            yv = ybd[:].rearrange("p b d -> p (b d)")
            for n in range(2 * NHB):
                if n >= 4:
                    pe.wait_ge(mixed, n - 3)
                nc.tensor.matmul(P[n % 4][0:T, :], RT[:, n // 2, 0:T], yv[:, (n % 2) * 512:(n % 2 + 1) * 512],
                                 start=True, stop=True).then_inc(mix_mm, 1)

        @block.scalar
        def _(act):
            def gate_acts(c, k, first):
                for g, (dst, func) in enumerate(((zg, ACT.Tanh), (fg, ACT.Sigmoid), (og, ACT.Sigmoid))):
                    act.wait_ge(gate_mm, 3 * c + g + 1)
                    if not first and g == 0:
                        act.wait_ge(h_ready, c - 1)
                        act.wait_ge(hR_ready, c - 1)
                    nc.scalar.activation(dst[:, k], PG[g][:, 0:CW], func).then_inc(gate_act, 1)

            def copy_xT(c, k, first):
                act.wait_ge(x_transposed, c + 1)
                if not first:
                    act.wait_ge(gate_mm, 3 * c - 3)
                nc.scalar.copy(xT[:, k], PX[:, 0:XW]).then_inc(xT_ready, 1)

            def copy_H(c):
                act.wait_ge(h_transposed, c + 1)
                nc.scalar.copy(H[0:T, bass.ds(c * CB, CB)].rearrange("p b c -> p (b c)") if not isinstance(c, int)
                               else H[0:T, c * CB:(c + 1) * CB].rearrange("p b c -> p (b c)"),
                               PH[0:T, :]).then_inc(H_ready, 1)

            def copy_w1T(e):
                act.wait_ge(w1_transposed, e + 1)
                nc.scalar.copy(w1T[:, bass.ds(e * FF, FF)] if not isinstance(e, int) else w1T[:, e * FF:(e + 1) * FF],
                               PW[:, :]).then_inc(w1T_ready, 1)

            copy_xT(0, 0, True)
            act.wait_ge(filt_mm, 1)
            nc.scalar.copy(gateT[:], PW[:, 256:256 + E])
            nc.scalar.copy(abT[:].rearrange("p a c -> p (a c)"), PW[0:ORDER, 0:256]).then_inc(filt_ev, 1)
            copy_xT(1, 1, True)
            gate_acts(0, 0, True)
            copy_xT(2, 0, False)
            gate_acts(1, 1, True)
            copy_H(0)
            copy_w1T(0)
            for c in range(2, 4):
                copy_xT(c + 1, (c + 1) % 2, False)
                gate_acts(c, c % 2, False)
                copy_H(c - 1)
                copy_w1T(c - 1)
            with act.Fori(1, NCH // 4 - 1) as i:
                for k in range(4):
                    c = i * 4 + k
                    copy_xT(c + 1, (k + 1) % 2, False)
                    gate_acts(c, k % 2, False)
                    copy_H(c - 1)
                    copy_w1T(c - 1)
            for c in range(NCH - 4, NCH):
                if c + 1 < NCH:
                    copy_xT(c + 1, (c + 1) % 2, False)
                gate_acts(c, c % 2, False)
                copy_H(c - 1)
                copy_w1T(c - 1)
            copy_H(NCH - 1)
            copy_w1T(NCH - 1)

            for g in range(NCG):
                act.wait_ge(conv_mm, g + 1)
                if g >= 2:
                    act.wait_ge(H_added, g - 1)
                nc.scalar.activation(gl[0:T, g % 2].rearrange("p c b -> p (c b)"), PG[g % 3][0:T, :],
                                     ACT.Gelu_apprx_tanh).then_inc(gelu_done, 1)

            for n in range(2 * NHB):
                act.wait_ge(x2_transposed, n + 1)
                if n >= 2:
                    act.wait_ge(logits_mm, n - 1)
                nc.scalar.copy(x2T[:, n % 2].rearrange("p b t -> p (b t)"), PR[n % 2][:, 0:4 * T]).then_inc(x2T_ready, 1)

            act.wait_ge(diff_ready, 1)
            nc.scalar.activation(wgt[0:T, 1], wgt[0:T, 0], ACT.Sigmoid)
            nc.scalar.activation(wgt[0:T, 2], wgt[0:T, 0], ACT.Sigmoid, scale=-1.0).then_inc(wgt_ready, 1)
            for g in range(NHB):
                act.wait_ge(tail_mm, g + 1)
                nc.scalar.copy(RT[:, g, 0:T], P[6 + g % 2][:, 0:T]).then_inc(tail_ev, 1)

            def copy_GT(n, k, first):
                act.wait_ge(g_transposed, n + 1)
                if not first:
                    act.wait_ge(expert_mm, n - 1)
                nc.scalar.copy(GT[:, k % 2], P[4 + k % 2][:, 0:SLOT]).then_inc(GT_ready, 1)

            def silu(n, k, first):
                act.wait_ge(expert_mm, n + 1)
                if not first:
                    act.wait_ge(esum_step, n - 3)
                nc.scalar.activation(S[:, k % 4], P[k % 4][:, :], ACT.Silu).then_inc(silu_done, 1)

            for n in range(12):
                copy_GT(n, n, n < 2)
                if n >= 2:
                    silu(n - 2, n - 2, n - 2 < 4)
            with act.Fori(1, NT // 12) as i:
                for k in range(12):
                    copy_GT(i * 12 + k, k, False)
                    silu(i * 12 + (k - 2), (k - 2) % 12, False)
            for n in range(NT // 12 * 12, NT):
                copy_GT(n, n, False)
                silu(n - 2, (n - 2) % 12, False)
            for n in range(NT - 2, NT):
                silu(n, n % 12, False)

            act.wait_ge(tail_mm, NHB + 1)
            nc.scalar.copy(yT[:], P[4][0:E, 0:128]).then_inc(tail_ev, 1)
            act.wait_ge(tail_mm, NHB + 2)
            for b in range(HB):
                a = nc.scalar.mul(ybd[:, b], P[5][:, 0:128], bmask[:, b:b + 1])
            a.then_inc(tail_ev, 1)

        @block.vector
        def _(dve):
            v = nc.vector

            def moments(st, m, ve, done, count, ready):
                v.tensor_tensor(m[:, 1], st[:, :, 1], st[:, :, 4], ALU.subtract)
                v.tensor_tensor(m[:, 2], st[:, :, 2], st[:, :, 5], ALU.add)
                v.tensor_tensor(m[:, 0], st[:, :, 1], st[:, :, 4], ALU.add).then_inc(done, 1)
                dve.wait_ge(done, count + 1)
                v.scalar_tensor_tensor(out=m[:, 1], in0=m[:, 1], scalar=0.25, in1=m[:, 1],
                                       op0=ALU.mult, op1=ALU.mult)
                v.tensor_scalar(m[:, 2], m[:, 2], 1.0 / D, EPS, ALU.mult, ALU.add).then_inc(done, 1)
                dve.wait_ge(done, count + 2)
                v.tensor_scalar(m[:, 0], m[:, 0], 0.5, None, ALU.mult).then_inc(done, 1)
                v.tensor_tensor(ve, m[:, 1], m[:, 2], ALU.add).then_inc(ready, 1)

            def cell(c, k):
                dve.wait_ge(gate_act, 3 * c + 3)
                if not (isinstance(c, int) and c < 2):
                    dve.wait_ge(hR_ready, c - 1)
                v.scalar_tensor_tensor(out=cc[:, k], in0=fg[:, k], scalar=-1.0, in1=zg[:, k],
                                       op0=ALU.add, op1=ALU.mult).then_inc(cell_step, 1)
                dve.wait_ge(cell_step, 3 * c + 1)
                v.memset(fg[:, k].rearrange("p (b t) -> p b t", b=CB)[:, :, 0:1], 0.0).then_inc(cell_step, 1)
                dve.wait_ge(cell_step, 3 * c + 2)
                v.tensor_tensor_scan(cc[:, k], fg[:, k], cc[:, k], 0.0, ALU.mult, ALU.subtract).then_inc(cell_step, 1)
                dve.wait_ge(cell_step, 3 * c + 3)
                if not (isinstance(c, int) and c < 2):
                    dve.wait_ge(h_transposed, c - 1)
                v.tensor_tensor(hT[:, k], cc[:, k], og[:, k], ALU.mult).then_inc(h_ready, 1)

            def stats(c, k):
                dve.wait_ge(h_transposed, c + 1)
                for q in range(CB):
                    a = v.bn_stats(st1[0:T, k, q], PR[k][0:T, q * D:(q + 1) * D])
                a.then_inc(bn1, 1)
                dve.wait_ge(bn1, 4 * c + 1)
                moments(st1[0:T, k], mm1[0:T, k], ve1[0:T, k], bn1, 4 * c + 1, ve1_ready)

            def norm(c, k):
                dve.wait_ge(rstd1, c + 1)
                for q in range(CB):
                    at = c * CB + q
                    dst = XN[0:T, at] if isinstance(at, int) else XN[0:T, bass.ds(at, 1)].rearrange("p a c -> p (a c)")
                    a = v.tensor_scalar(dst, PR[k][0:T, q * D:(q + 1) * D], mm1[0:T, k, 0, q:q + 1], rs1[0:T, k, q:q + 1],
                                        ALU.subtract, ALU.mult)
                a.then_inc(xn1_ready, 1)

            cell(0, 0)
            steps = [0]

            def fstep(ins):
                steps[0] += 1
                ins.then_inc(filt_step, 1)
                dve.wait_ge(filt_step, steps[0])

            dve.wait_ge(filt_mm, 2)
            fstep(v.tensor_copy(fr[:, 0:4].rearrange("p a c -> p (a c)"), PW[0:NF, :]))
            fstep(v.tensor_scalar(fr[:, 2], fr[:, 2], 1.0, None, ALU.add))
            fstep(v.tensor_tensor(fr[:, 4:6], fr[:, 2:4], fr[:, 2:4], ALU.mult))
            fstep(v.tensor_tensor(fr[:, 6], fr[:, 4], fr[:, 5], ALU.add))
            fstep(v.reciprocal(fr[:, 7], fr[:, 6]))
            v.tensor_tensor(fr[:, 4], fr[:, 0], fr[:, 2], ALU.mult)
            v.tensor_tensor(fr[:, 5], fr[:, 1], fr[:, 3], ALU.mult)
            v.tensor_tensor(fr[:, 8], fr[:, 1], fr[:, 2], ALU.mult)
            fstep(v.tensor_tensor(fr[:, 9], fr[:, 0], fr[:, 3], ALU.mult))
            fstep(v.tensor_tensor(fr[:, 4], fr[:, 4], fr[:, 5], ALU.add))
            fstep(v.tensor_tensor(fr[:, 8], fr[:, 8], fr[:, 9], ALU.subtract))
            fstep(v.tensor_tensor(fr[:, 10], fr[:, 4], fr[:, 7], ALU.mult))
            fstep(v.tensor_tensor(fr[:, 11], fr[:, 8], fr[:, 7], ALU.mult))
            steps[0] += 1
            v.tensor_copy(fr[:, 6], fr[:, 7]).then_inc(filt_step, 1)
            dve.wait_ge(filt_step, steps[0])
            cell(1, 1)
            dve.wait_ge(filt_mm, 3)
            dve.wait_ge(pool_const, 1)
            dve.wait_ge(ab_in, 96)
            v.tensor_copy(kp[:, T:2 * T - 1], PW[:, 1:T])
            v.tensor_scalar(kp[:, T - 1:T], PW[:, 0:1], h0c[:, 0:1], None, ALU.add).then_inc(filt_step, 1)
            assert steps[0] + 1 == FILT_LAST, steps[0]
            stats(0, 0)
            for c in range(2, 4):
                cell(c, c % 2)
                stats(c - 1, (c - 1) % 2)
                norm(c - 2, c % 2)
            with dve.Fori(1, NCH // 4) as i:
                for k in range(4):
                    c = i * 4 + k
                    cell(c, k % 2)
                    stats(c - 1, (k + 1) % 2)
                    norm(c - 2, k % 2)
            stats(NCH - 1, (NCH - 1) % 2)
            norm(NCH - 2, NCH % 2)
            norm(NCH - 1, (NCH - 1) % 2)

            dve.wait_ge(H_ready, NCH)
            with dve.Fori(0, NCG // 2) as i:
                for k in range(2):
                    g = i * 2 + k
                    dve.wait_ge(gelu_done, g + 1)
                    hv = H[0:T, :, bass.ds(g * CG, CG)].rearrange("p b c -> p c b")
                    v.tensor_tensor(hv, hv, gl[0:T, k], ALU.add).then_inc(H_added, 1)
            dve.wait_ge(H_added, NCG)

            def norm2(g):
                dve.wait_ge(rstd2, g + 1)
                for q in range(HB):
                    b = g * HB + q
                    a = v.tensor_scalar(XN[0:T, b], H[0:T, b], mm2[0:T, g % 2, 0, q:q + 1], rs2[0:T, g % 2, q:q + 1],
                                        ALU.subtract, ALU.mult)
                a.then_inc(xn2_ready, 1)

            for g in range(NHB):
                for q in range(HB):
                    a = v.bn_stats(st2[0:T, g % 2, q], H[0:T, g * HB + q])
                a.then_inc(bn2, 1)
                dve.wait_ge(bn2, 4 * g + 1)
                moments(st2[0:T, g % 2], mm2[0:T, g % 2], ve2[0:T, g % 2], bn2, 4 * g + 1, ve2_ready)
                if g >= 1:
                    norm2(g - 1)
            norm2(NHB - 1)

            rs = [0]

            def step(ins):
                rs[0] += 1
                ins.then_inc(route_step, 1)
                dve.wait_ge(route_step, rs[0])

            v.memset(esum[:, :], 0.0).then_inc(esum_clear, 1)
            dve.wait_ge(logits_mm, 2 * NHB)
            dve.wait_ge(const_in, 32)
            for h in range(2):
                a = v.tensor_copy(L[0:T, h * 32:(h + 1) * 32].rearrange("p b e -> p (b e)"), P[h][0:T, :])
            step(a)

            def per_b(n):
                return mx[0:T, n].unsqueeze(2).to_broadcast([T, B, E])

            rk = rank_sb[0:T].unsqueeze(1).to_broadcast([T, B, E])
            src = L
            for k in range(2):
                step(v.tensor_reduce(mx[0:T, k], src[0:T], AX.X, ALU.max))
                step(v.tensor_tensor(OH[k][0:T], src[0:T], per_b(k), ALU.is_equal))
                step(v.tensor_tensor(OH[k][0:T], OH[k][0:T], rk, ALU.mult))
                step(v.tensor_reduce(mx[0:T, 2 + k], OH[k][0:T], AX.X, ALU.max))
                step(v.tensor_tensor(OH[k][0:T], rk, per_b(2 + k), ALU.is_equal))
                if k == 0:
                    step(v.scalar_tensor_tensor(out=LW[0:T], in0=OH[0][0:T], scalar=NEG, in1=L[0:T],
                                                op0=ALU.mult, op1=ALU.add))
                    src = LW
            v.tensor_tensor(wgt[0:T, 0], mx[0:T, 0], mx[0:T, 1], ALU.subtract).then_inc(diff_ready, 1)
            v.tensor_tensor(maskb[0:T].rearrange("p (b e) -> p b e", b=B), OH[0][0:T], OH[1][0:T],
                            ALU.add).then_inc(mask_ready, 1)
            dve.wait_ge(prefix_mm, 1)
            for h in range(2):
                a = v.tensor_copy(tot[:, :, h * 32:(h + 1) * 32],
                                  P[2 + h][:, :].rearrange("p (b e) -> p e b", b=32))
            step(a)
            flat = tot.rearrange("p e b -> p (e b)")
            step(v.tensor_tensor_scan(cum.rearrange("p e b -> p (e b)"), flat, flat, 0.0, ALU.add, ALU.max))
            step(v.tensor_copy(small[:, 0], cum[:, :, B - 1]))
            v.tensor_copy(small[:, 1, 0:1], small[:, 0, 0:1])
            step(v.tensor_tensor(small[:, 1, 1:E], small[:, 0, 1:E], small[:, 0, 0:E - 1], ALU.subtract))
            step(v.tensor_scalar(smi[:, 0], small[:, 1], float(SLOT - 1), None, ALU.add))
            step(v.tensor_scalar(smi[:, 1], smi[:, 0], 7, None, ALU.arith_shift_right))
            step(v.tensor_copy(small[:, 4], smi[:, 1]))
            step(v.tensor_tensor_scan(small[:, 2], small[:, 4], small[:, 4], 0.0, ALU.add, ALU.max))
            v.tensor_scalar(small[:, 3, 0:1], small[:, 0, 0:1], 0.0, None, ALU.mult)
            step(v.scalar_tensor_tensor(out=small[:, 3, 1:E], in0=small[:, 2, 0:E - 1], scalar=float(SLOT),
                                        in1=small[:, 0, 0:E - 1], op0=ALU.mult, op1=ALU.subtract))
            step(v.tensor_tensor(cum[:], cum[:], tot[:], ALU.subtract))
            step(v.tensor_tensor(cum[:], cum[:], small[:, 3].unsqueeze(2).to_broadcast([128, E, B]), ALU.add))
            for h in range(2):
                a = v.tensor_tensor(LW[0:T, h * 32:(h + 1) * 32],
                                    P[h][0:T, :].rearrange("p (b e) -> p b e", b=32),
                                    cum[0:T, :, h * 32:(h + 1) * 32].rearrange("p e b -> p b e"), ALU.add)
            step(a)
            for k in range(2):
                step(v.tensor_tensor(tot[0:T].rearrange("p e b -> p (e b)").rearrange("p (b e) -> p b e", b=B),
                                     LW[0:T], OH[k][0:T], ALU.mult))
                step(v.tensor_reduce(pos[0:T, k * B:(k + 1) * B],
                                     tot[0:T].rearrange("p e b -> p (e b)").rearrange("p (b e) -> p b e", b=B),
                                     AX.X, ALU.add))
            step(v.tensor_copy(posi[0:T, 0], pos[0:T]))
            v.tensor_scalar(posi[0:T, 1], posi[0:T, 0], 7, None, ALU.arith_shift_right)
            step(v.tensor_scalar(posi[0:T, 2], posi[0:T, 0], SLOT - 1, None, ALU.bitwise_and))
            step(v.tensor_copy(hilo[0:T], posi[0:T, 1:3]))

            dve.wait_ge(pool_const, 2)
            for n in range(2 * B):
                if n >= 4:
                    dve.wait_ge(code_mm, n - 3)
                v.tensor_scalar(ohl[0:T, n % 4], iotb[0:T, 0:128], hilo[0:T, 1, n:n + 1], None, ALU.is_equal)
                v.tensor_scalar(ohh[0:T, n % 4, 0:NT], iotb[0:T], hilo[0:T, 0, n:n + 1], code_sb[0:T, n % B:n % B + 1],
                                ALU.is_equal, ALU.mult).then_inc(onehot, 1)
            dve.wait_ge(code_mm, 2 * B)
            step(v.tensor_scalar(idx[:], P[4][:, 0:NT].bitcast(I32), 16, None, ALU.arith_shift_right))
            step(v.tensor_scalar(idx[:], idx[:], float((127 - EXPO - 1) * 128), 0.0, ALU.subtract, ALU.max))
            step(v.tensor_scalar(idx2[:], idx[:], 7, None, ALU.arith_shift_right))
            step(v.scalar_tensor_tensor(out=idx[:], in0=idx2[:], scalar=float(T - 128), in1=idx[:],
                                        op0=ALU.mult, op1=ALU.add))
            v.tensor_scalar(idx[:], idx[:], float(T - 1), 0.0, ALU.subtract, ALU.max).then_inc(idx_ready, 1)
            step(v.memset(eidf[:], 0.0))
            for e in range(E - 1):
                step(v.scalar_tensor_tensor(out=eidf[:, (e + 1) % 2], in0=iotb[0:1, :], scalar=small[0:1, 2, e:e + 1],
                                            in1=eidf[:, e % 2], op0=ALU.is_ge, op1=ALU.add))
            v.tensor_copy(eid[:], eidf[:, (E - 1) % 2]).then_inc(eid_ready, 1)
            dve.wait_ge(wgt_ready, 1)
            for k in range(2):
                step(v.tensor_tensor(OH[k][0:T], OH[k][0:T],
                                     wgt[0:T, 1 + k].unsqueeze(2).to_broadcast([T, B, E]), ALU.mult))
            v.tensor_tensor(L[0:T], OH[0][0:T], OH[1][0:T], ALU.add).then_inc(R_ready, 1)
            step(v.tensor_scalar(small[:, 5], small[:, 1], 1.0, None, ALU.max))
            step(v.reciprocal(small[:, 6], small[:, 5]))

            dve.wait_ge(esum_clear, 1)
            dve.wait_ge(eid_ready, 1)

            def accumulate(n, k, first):
                e = dve.value_load(eid[0:1, bass.ds(n, 1)], min_val=0, max_val=E - 1)
                dve.wait_ge(silu_done, n + 1)
                if not first:
                    dve.wait_ge(esum_step, n)
                at = esum[:, bass.ds(e * FF, FF)]
                v.tensor_tensor(at, at, S[:, k % 4], ALU.add).then_inc(esum_step, 1)

            for n in range(12):
                accumulate(n, n, n == 0)
            with dve.Fori(1, NT // 12) as i:
                for k in range(12):
                    accumulate(i * 12 + k, k, False)
            for n in range(NT // 12 * 12, NT):
                accumulate(n, n, False)

            dve.wait_ge(w2_in, 16)
            for e in range(E):
                dve.wait_ge(hsum_mm, e + 1)
                if e >= 1:
                    dve.wait_ge(y_step, e)
                v.tensor_tensor_reduce(out=junk[:], in0=w2_sb[:, e], in1=P[e % 4][:, :], scale=1.0, scalar=0.0,
                                       op0=ALU.mult, op1=ALU.add, accum_out=y[:, 0, e:e + 1]).then_inc(y_step, 1)
            dve.wait_ge(y_step, E)
            v.tensor_tensor(y[:, 1], y[:, 0], small[:, 6], ALU.mult).then_inc(y_step, 1)
            for n in range(2 * NHB):
                dve.wait_ge(mix_mm, n + 1)
                hv = H[0:T, 4 * n:4 * (n + 1)].rearrange("p b c -> p (b c)")
                v.tensor_tensor(hv, P[n % 4][0:T, :], hv, ALU.add).then_inc(mixed, 1)


_INS = ["x", "L0_tok_kernel", "L0_attn_A", "L0_attn_B", "L0_attn_h0", "L0_ffn_gate_weight", "L0_ffn_w1", "L0_ffn_w2"]


def kernel(**inputs):
    import numpy as _np
    import concourse.bacc as _bacc
    from concourse import mybir as _mybir
    from concourse.bass_utils import run_bass_kernel_spmd as _run

    nc = _bacc.Bacc("TRN2", target_bir_lowering=False, num_devices=1)
    arrays, args = {}, []
    for name in _INS:
        arrays[f"in_{name}"] = _np.ascontiguousarray(inputs[name])
    for name, a in tables().items():
        arrays[f"const_{name}"] = a
    for name, a in arrays.items():
        args.append(nc.dram_tensor(name, a.shape, _mybir.dt.from_np(a.dtype), kind="ExternalInput").ap())
    args.append(nc.dram_tensor("out", (B, T, D), FP32, kind="ExternalOutput").ap())
    args.append(nc.dram_tensor("kpad", (D, KROW), FP32, kind="Internal").ap())
    args.append(nc.dram_tensor("table", (NTOK + 1, D), FP32, kind="Internal").ap())
    build(nc, *args)
    return _run(nc, [arrays], core_ids=[0]).results[0]["out"]
```

```python
from contextlib import ExitStack

import numpy as np

import concourse.bass as bass
from concourse import mybir

FP32 = mybir.dt.float32
FP32R = mybir.dt.float32r
BF16 = mybir.dt.bfloat16
I32 = mybir.dt.int32
ALU = mybir.AluOpType
ACT = mybir.ActivationFunctionType
AX = mybir.AxisListType

B, TIN, D = 64, 125, 128
WIN = 3
T = TIN - WIN + 1
ORDER = 64
NF = T // 2 + 1
E, FF = 16, 512
EPS = 1e-5

CB = 4
NCH = B // CB
CW = CB * T
XW = CB * TIN
NV = XW - WIN + 1
XBUF = 4

CG = 8
NCG = D // CG
HP = 8
NHP = D // HP
HRES = 12
KROW = 256
WARM = 112
HB = 8
NHB = B // HB
ACT_NORM = 3

SLOT = 128
NTOK = B * T
NT = (2 * NTOK + E * (SLOT - 1)) // SLOT
UNROLL = 12
GBUF = 6
OBUF = 8
ON_ACT, ON_POOL = (1, 4, 7), (2, 5, 6)
assert NT % GBUF == 0 and NT <= 256
SPLIT = 112

EXPO = 32
NEG = -3.0e38
ARENA = 10128


def tables():
    n = np.arange(ORDER, dtype=np.float64)[:, None]
    k = np.arange(NF, dtype=np.float64)[None, :]
    w = 2 * np.pi * k / T
    m = np.arange(T, dtype=np.float64)[None, :]
    half = np.where(np.arange(NF) == 0, 1.0, 2.0)[:, None] / T
    ph = 2 * np.pi * k.T * m / T
    out = {
        "dft": np.concatenate([np.cos(w * n), -np.sin(w * n), np.cos(w * (n + 1)), -np.sin(w * (n + 1))], 1),
        "idft": np.concatenate([half * np.cos(ph), -half * np.sin(ph)], 1),
        "code": (1 + np.arange(128)[:, None] / 128.0) * 2.0 ** (np.arange(B)[None, :] - EXPO),
        "rank": np.tile(E - np.arange(E)[None, :], (128, 1)),
    }
    return {k: v.astype(np.float32) for k, v in out.items()}


def build(nc, x, wconv, fa, fb, h0, gate, w1, w2, dft, idft, code, rank, out, kpad, table):
    ctx = ExitStack()

    def sb(name, shape, dt=FP32):
        return ctx.enter_context(nc.sbuf_tensor(name, shape, dt))

    def pb(name):
        return ctx.enter_context(nc.psum_tensor(name, [128, 512], FP32))

    def sem(name):
        return ctx.enter_context(nc.semaphore(name))

    with ctx:
        BIG = sb("BIG", [128, 3 * E * FF // 2])
        hank = BIG[:, 0:HRES * HP * T].rearrange("p (q c t) -> p q c t", q=HRES, c=HP)
        esum = BIG[:, 0:E * FF]
        w1T = sb("w1T", [128, E * FF])
        H = sb("H", [128, B, D])
        XN = sb("XN", [128, B, D])
        XF = XN[:].rearrange("p b c -> p (b c)")
        XC = XN[:].rearrange("p b c -> p (b c)").rearrange("p (c b) -> p c b", c=D)
        w2_sb = XN[:].rearrange("p b c -> p (b c)").rearrange("p (e f) -> p e f", e=E)
        wh = sb("wh", [128, WIN, 3 * D], FP32R)
        wl = sb("wl", [128, WIN, 3 * D], FP32R)
        xh = sb("xh", [128, 2, XW], FP32R)
        xl = sb("xl", [128, 2, XW], FP32R)
        arena = sb("arena", [128, ARENA])
        used = [0]

        def carve(*dims, dt=FP32):
            n = int(np.prod(dims))
            words = n if dt != BF16 else (n + 1) // 2
            part = arena[:, used[0]:used[0] + words]
            used[0] += words
            assert used[0] <= ARENA, used[0]
            if dt != FP32:
                part = part.bitcast(dt)[:, 0:n]
            if len(dims) == 2:
                part = part.rearrange("p (a b) -> p a b", a=dims[0])
            if len(dims) == 3:
                part = part.rearrange("p (a b c) -> p a b c", a=dims[0], b=dims[1])
            return part

        wk = carve(WIN, 3 * D)
        xin = carve(XBUF, CB, D)
        w1in = carve(2, 4, D)
        zg = carve(2, CW)
        fg = carve(2, CW)
        og = carve(2, CW)
        cc = carve(2, CW)
        hT = carve(2, CW)
        hR = carve(2, CW)
        used[0] = 0
        gl = carve(2, CG, B)
        x2T = carve(2, 4, T)
        L = carve(B, E)
        LW = carve(B, E)
        cum = carve(E, B)
        tot = carve(E, B)
        G = carve(GBUF, D)
        posi = carve(3, 2 * B, dt=I32)
        hilo = carve(2, 2 * B)
        nlo = carve(2 * B)
        GT = carve(2, SLOT)
        st2 = carve(2, HB * 6).rearrange("p a (q n) -> p a q n", q=HB)
        small = carve(7, E)
        y = carve(2, E)
        at = E * FF
        OHS = BIG[:, at:at + 2 * B * E].rearrange("p (k b e) -> p k b e", k=2, b=B)
        OH = [OHS[:, 0], OHS[:, 1]]
        at += 2 * B * E
        maskb = BIG[:, at:at + B * E // 2].bitcast(BF16)
        at += B * E // 2
        ohl = BIG[:, at:at + OBUF * 64].bitcast(BF16).rearrange("p (k n) -> p k n", k=OBUF)
        at += OBUF * 64
        ohh = BIG[:, at:at + OBUF * (NT // 2)].bitcast(BF16).rearrange("p (k n) -> p k n", k=OBUF)
        ohq = BIG[:, at + OBUF * (NT // 2):at + OBUF * (NT // 2) + 128].bitcast(BF16).rearrange("p (k n) -> p k n", k=2)
        S = OHS.rearrange("p a b e -> p (a b e)").rearrange("p (k f) -> p k f", k=4)
        RT = x2T.rearrange("p a b t -> p (a b) t")
        gl0 = gl[:, 0].rearrange("p c b -> p (c b)")
        gl1 = gl[:, 1].rearrange("p c b -> p (c b)")
        mx = gl0[:, 0:4 * B].rearrange("p (n b) -> p n b", n=4)
        pos = gl0[:, 4 * B:6 * B]
        wgt = gl1[:, 0:3 * B].rearrange("p (n b) -> p n b", n=3)
        idx = gl1[:, 3 * B:3 * B + NT].bitcast(I32)
        junk = gl0
        idx2 = GT.rearrange("p k s -> p (k s)")[:, 0:NT].bitcast(I32)
        lw = LW.rearrange("p b e -> p (b e)")
        ends = gl1[0:E - 1, 3 * B + NT:3 * B + 2 * NT]
        eid = lw[0:1, 0:NT].bitcast(I32)
        yT = lw[0:E, NT:NT + D]
        ybd = cum.rearrange("p e b -> p (e b)").rearrange("p (b d) -> p b d", b=HB)

        st1 = sb("st1", [128, 2, CB, 6])
        mm1 = sb("mm1", [128, 2, 3, CB])
        ve1 = sb("ve1", [128, 2, CB])
        rs1 = sb("rs1", [128, 2, CB])
        mhalf = sb("mhalf", [128, HB])
        ident = sb("ident", [128, 128])
        fr = w1T[0:NF, 12 * FF:15 * FF].rearrange("p (a c) -> p a c", a=12)
        dft_sb = w1T[0:ORDER, 15 * FF:15 * FF + 4 * NF]
        idft_sb = w1T[0:NF, 15 * FF + 4 * NF:15 * FF + 4 * NF + 2 * T]
        ab = XN[:, B - 1].rearrange("p (a n) -> p a n", a=2)
        gate_in = XN[0:E, B - 4]
        kp = H[:, B - 2:B].rearrange("p a n -> p (a n)")
        abT = XN[0:ORDER, B - 3:B - 1]
        code_sb = sb("code_sb", [128, B])
        rank_sb = sb("rank_sb", [128, E])
        h0c = sb("h0c", [128, 1])
        gateT = sb("gateT", [128, WARM])
        mm2 = sb("mm2", [128, 2, 3, HB])
        ve2 = sb("ve2", [128, 2, HB])
        rs2 = sb("rs2", [128, 2, HB])
        nmr = sb("nmr", [128, 2, HB])
        trib = sb("trib", [128, 128], BF16)
        oneb = sb("oneb", [128, 128], BF16)
        smi = sb("smi", [128, 2, E], I32)
        iotb = sb("iotb", [128, NT], BF16)
        rep = sb("rep", [E, 128])
        bmask = sb("bmask", [128, HB])
        onef = sb("onef", [128, 128])

        P = [pb(f"P{n}") for n in range(8)]
        PG, PX, PH, PR, PW = P[0:3], P[3], P[4], P[5:7], P[7]

        const_in = sem("const_in")
        wk_in = sem("wk_in")
        ab_in = sem("ab_in")
        x_in = [sem(f"x_in{n}") for n in range(XBUF)]
        w1_in = [sem(f"w1_in{n}") for n in range(2)]
        w2_in = sem("w2_in")
        kpad_out = sem("kpad_out")
        hank_in = [sem(f"hank_in{n}") for n in range(NHP)]
        table_out = sem("table_out")
        zero_out = sem("zero_out")
        out_done = sem("out_done")
        pool_const = sem("pool_const")
        pool_step = sem("pool_step")
        ident_ok = sem("ident_ok")
        x_transposed = sem("x_transposed")
        xh_ready = sem("xh_ready")
        xl_ready = sem("xl_ready")
        wsplit = sem("wsplit")
        gate_mm = sem("gate_mm")
        gate_act = sem("gate_act")
        w1_transposed = sem("w1_transposed")
        w1T_ready = sem("w1T_ready")
        cell_step = sem("cell_step")
        h_ready = sem("h_ready")
        hR_ready = sem("hR_ready")
        h_transposed = sem("h_transposed")
        H_ready = sem("H_ready")
        bn1 = sem("bn1")
        ve1_ready = sem("ve1_ready")
        rstd1 = sem("rstd1")
        xn1_ready = sem("xn1_ready")
        filt_mm = sem("filt_mm")
        filt_ev = sem("filt_ev")
        filt_step = sem("filt_step")
        conv_mm = sem("conv_mm")
        gelu_done = sem("gelu_done")
        H_added = sem("H_added")
        bn2 = sem("bn2")
        ve2_ready = sem("ve2_ready")
        rstd2 = sem("rstd2")
        xn2_ready = sem("xn2_ready")
        nmr_ready = sem("nmr_ready")
        xn2_act = sem("xn2_act")
        x2_transposed = sem("x2_transposed")
        x2T_ready = sem("x2T_ready")
        logits_mm = sem("logits_mm")
        route_step = sem("route_step")
        mask_ready = sem("mask_ready")
        prefix_mm = sem("prefix_mm")
        diff_ready = sem("diff_ready")
        wgt_ready = sem("wgt_ready")
        hilo_ready = sem("hilo_ready")
        onehot = sem("onehot")
        onehot_act = sem("onehot_act")
        onehot_pool = sem("onehot_pool")
        act_square = sem("act_square")
        L_ready = sem("L_ready")
        code_mm = sem("code_mm")
        idx_ready = sem("idx_ready")
        ends_ready = sem("ends_ready")
        eid_mm = sem("eid_mm")
        eid_ready = sem("eid_ready")
        esum_clear = sem("esum_clear")
        gathered = [sem(f"gathered{n}") for n in range(GBUF)]
        g_transposed = sem("g_transposed")
        GT_ready = sem("GT_ready")
        expert_mm = sem("expert_mm")
        silu_done = sem("silu_done")
        esum_step = sem("esum_step")
        hsum_mm = sem("hsum_mm")
        y_step = sem("y_step")
        R_ready = sem("R_ready")
        tail_mm = sem("tail_mm")
        tail_ev = sem("tail_ev")
        mix_mm = sem("mix_mm")
        mixed = sem("mixed")
        ybd_dve = sem("ybd_dve")

        xr = x.rearrange("(n b) t d -> n t b d", b=CB)
        w1r = w1.rearrange("e (q p) d -> e p q d", p=128)
        FILT_EV, FILT_LAST = 4, 12

        def share(n, mine):
            return sum(m % OBUF in mine for m in range(n))

        def hankel(q):
            return bass.AP(kpad.tensor, q * HP * KROW, [[1, 128], [KROW, HP], [1, T]])

        block = ctx.enter_context(nc.Block())

        @block.sync
        def _(sp):
            sp.dma_start(xin[0:TIN, 0], xr[0]).then_inc(x_in[0], 16)
            sp.dma_start(wk[:], wconv.rearrange("w d n -> d w n")).then_inc(wk_in, 16)
            sp.dma_start(xin[0:TIN, 1], xr[1]).then_inc(x_in[1], 16)
            sp.dma_start(ab[:, 0], fa).then_inc(ab_in, 16)
            sp.dma_start(ab[:, 1], fb).then_inc(ab_in, 16)
            sp.dma_start(dft_sb[:], dft).then_inc(ab_in, 16)
            sp.dma_start(idft_sb[:], idft).then_inc(ab_in, 16)
            sp.dma_start(h0c[:], bass.AP(h0.tensor, 0, [[0, 128], [1, 1]])).then_inc(ab_in, 16)
            sp.dma_start(gate_in[:], gate).then_inc(ab_in, 16)
            for n in range(2, XBUF):
                sp.dma_start(xin[0:TIN, n], xr[n]).then_inc(x_in[n], 16)
            sp.dma_start(code_sb[:], code).then_inc(const_in, 16)
            sp.dma_start(rank_sb[:], rank).then_inc(const_in, 16)
            for n in range(2):
                sp.dma_start(w1in[:, n], w1r[n]).then_inc(w1_in[n], 16)
            for c in range(2, NCH):
                sp.wait_ge(w1_transposed, c - 1)
                sp.dma_start(w1in[:, c % 2], w1r[c]).then_inc(w1_in[c % 2], 16)
                if c + 2 < NCH and c + 2 >= XBUF:
                    sp.wait_ge(x_transposed, c + 3 - XBUF)
                    sp.dma_start(xin[0:TIN, (c + 2) % XBUF], xr[c + 2]).then_inc(x_in[(c + 2) % XBUF], 16)
                if c == 3:
                    sp.wait_ge(kpad_out, 16)
                for q in range(max(c - 3, 0), min(c - 2, HRES)):
                    sp.dma_start(hank[:, q], hankel(q)).then_inc(hank_in[q], 16)
            for q in range(HRES, NHP):
                sp.wait_ge(conv_mm, (q - HRES + 1) * HP // CG)
                sp.dma_start(hank[:, q % HRES], hankel(q)).then_inc(hank_in[q], 16)
            tv = table[1:, :].rearrange("(b t) d -> t b d", t=T)
            for g in range(NHB):
                sp.wait_ge(xn2_ready, g + 1)
                sp.wait_ge(xn2_act, g + 1)
                for lo, hi in ((0, SPLIT), (SPLIT, T)):
                    sp.dma_start(tv[lo:hi, g * HB:(g + 1) * HB], XN[lo:hi, g * HB:(g + 1) * HB]).then_inc(table_out, 16)
            sp.wait_ge(table_out, 2 * NHB * 16)
            sp.wait_ge(x2_transposed, 2 * NHB)
            sp.dma_start(w2_sb, w2.rearrange("e d f -> d e f")).then_inc(w2_in, 16)
            sp.wait_ge(esum_clear, NHB)
            sp.dma_start(table[0:1, :], esum[0:1, 0:D]).then_inc(zero_out, 16)
            ov = out.rearrange("b t d -> t b d")
            for g in range(NHB):
                sp.wait_ge(mixed, 2 * (g + 1))
                for lo, hi in ((0, SPLIT), (SPLIT, T)):
                    sp.dma_start(ov[lo:hi, g * HB:(g + 1) * HB], H[lo:hi, g * HB:(g + 1) * HB]).then_inc(out_done, 16)
            sp.wait_ge(out_done, 2 * NHB * 16)

        @block.gpsimd
        def _(pool):
            pool.memset(onef[:], 1.0)
            pool.memset(oneb[:], 1.0)
            pool.memset(mhalf[:], -0.5)
            pool.memset(gateT[:], 0.0)
            pool.memset(kp[:], 0.0).then_inc(pool_const, 1)
            pool.wait_ge(pool_const, 1)
            pool.affine_select(out=ident[:], in_=onef[:], compare_op=ALU.is_equal, fill=0.0, base=0,
                               pattern=[[-1, 128]], channel_multiplier=1).then_inc(ident_ok, 1)
            pool.affine_select(out=trib[:], in_=onef[:], compare_op=ALU.is_gt, fill=0.0, base=0,
                               pattern=[[1, 128]], channel_multiplier=-1)
            pool.affine_select(out=rep[:].rearrange("p (b e) -> p b e", b=HB),
                               in_=onef[0:E, :].rearrange("p (b e) -> p b e", b=HB),
                               compare_op=ALU.is_equal, fill=0.0, base=0,
                               pattern=[[0, HB], [-1, E]], channel_multiplier=1)
            pool.affine_select(out=bmask[:], in_=onef[:, 0:HB], compare_op=ALU.is_ge, fill=0.0, base=0,
                               pattern=[[-E, HB]], channel_multiplier=1).then_inc(pool_step, 1)
            pool.wait_ge(pool_step, 1)
            pool.affine_select(out=bmask[:], in_=bmask[:], compare_op=ALU.is_gt, fill=0.0, base=E,
                               pattern=[[E, HB]], channel_multiplier=-1)
            pool.iota(iotb[:], pattern=[[1, NT]], base=0, channel_multiplier=0,
                      allow_small_or_imprecise_dtypes=True).then_inc(pool_const, 1)

            def reverse(c, k):
                pool.wait_ge(cell_step, 3 * c + 3)
                cv, ov, dst = (a[:, k].rearrange("p (b t) -> p b t", b=CB) for a in (cc, og, hR))
                nc.gpsimd.tensor_tensor(dst[:, :, ::-1], cv, ov, ALU.mult).then_inc(hR_ready, 1)

            def rstd(c, k):
                pool.wait_ge(ve1_ready, c + 1)
                nc.gpsimd.tensor_tensor(rs1[0:T, k], ve1[0:T, k], mhalf[0:T, 0:CB], ALU.pow).then_inc(rstd1, 1)

            for c in range(2):
                if c >= 1:
                    rstd(c - 1, (c - 1) % 2)
                reverse(c, c % 2)
            with pool.Fori(1, NCH // 2) as i:
                for k in range(2):
                    rstd(i * 2 + (k - 1), 1 - k)
                    pool.wait_ge(h_transposed, i * 2 + (k - 1))
                    reverse(i * 2 + k, k)
            rstd(NCH - 1, (NCH - 1) % 2)
            for g in range(NHB):
                pool.wait_ge(ve2_ready, g + 1)
                if g >= 2:
                    pool.wait_ge(xn2_ready, g - 1)
                    pool.wait_ge(xn2_act, g - 1)
                nc.gpsimd.tensor_tensor(rs2[0:T, g % 2], ve2[0:T, g % 2], mhalf[0:T], ALU.pow).then_inc(rstd2, 1)
                pool.memset(esum[:, g * E * FF // NHB:(g + 1) * E * FF // NHB], 0.0).then_inc(esum_clear, 1)
            pool.wait_ge(hilo_ready, 1)
            for n in range(2 * B):
                if n % OBUF in ON_POOL:
                    if n >= OBUF:
                        pool.wait_ge(code_mm, n - OBUF + 1)
                    nc.gpsimd.tensor_scalar(ohl[0:T, n % OBUF], iotb[0:T, 0:128], hilo[0:T, 1, n:n + 1], None,
                                            ALU.is_equal).then_inc(onehot_pool, 1)
            pool.wait_ge(idx_ready, 1)
            pool.wait_ge(table_out, 2 * NHB * 16)
            pool.wait_ge(zero_out, 16)
            for n in range(NT):
                if n >= GBUF:
                    pool.wait_ge(g_transposed, n - GBUF + 1)
                pool.indirect_dma_start(
                    out=G[:, n % GBUF, :], out_offset=None, in_=table[:, :],
                    in_offset=bass.IndirectOffsetOnAxis(ap=idx[:, n:n + 1], axis=0),
                ).then_inc(gathered[n % GBUF], 16)

        @block.tensor
        def _(pe):
            def x_transposes(c, k, nth):
                pe.wait_ge(x_in[k], 16 * (nth + 1))
                if not (isinstance(c, int) and c == 0):
                    pe.wait_ge(xl_ready, c)
                for q in range(CB):
                    mm = nc.tensor.transpose(PX[:, q * TIN:(q + 1) * TIN], xin[0:TIN, k, q], ident[0:TIN, 0:TIN])
                mm.then_inc(x_transposed, 1)

            def gates(c, k, first):
                pe.wait_ge(xl_ready, c + 1)
                for g in range(3):
                    if not first:
                        pe.wait_ge(gate_act, 3 * c - 3 + g + 1)
                    at, left = slice(g * D, (g + 1) * D), 3 * WIN
                    for w in range(WIN):
                        for wpart, xpart in ((wh, xh), (wh, xl), (wl, xh)):
                            left -= 1
                            mm = nc.tensor.matmul(PG[g][:, 0:NV], wpart[:, w, at], xpart[:, k, w:w + NV],
                                                  start=(left == 3 * WIN - 1), stop=(left == 0))
                    mm.then_inc(gate_mm, 1)

            def h_transposes(c, k, first, second):
                pe.wait_ge(h_ready, c + 1)
                pe.wait_ge(hR_ready, c + 1)
                if not first:
                    pe.wait_ge(H_ready, c)
                for q in range(CB):
                    nc.tensor.transpose(PH[0:T, q * D:(q + 1) * D], hT[:, k, q * T:(q + 1) * T], ident[:])
                if not (first or second):
                    pe.wait_ge(xn1_ready, c - 1)
                for q in range(CB):
                    mm = nc.tensor.transpose(PR[k][0:T, q * D:(q + 1) * D], hR[:, k, q * T:(q + 1) * T], ident[:])
                mm.then_inc(h_transposed, 1)

            def w1_transposes(e, k, nth, first):
                pe.wait_ge(w1_in[k], 16 * (nth + 1))
                if not first:
                    pe.wait_ge(w1T_ready, e)
                for q in range(4):
                    mm = nc.tensor.transpose(PW[:, q * 128:(q + 1) * 128], w1in[:, k, q], ident[:])
                mm.then_inc(w1_transposed, 1)

            def logits(n):
                pe.wait_ge(x2T_ready, n + 1)
                bank, at = P[n // 8], (n % 8) * 64
                for q in range(4):
                    lo = at + q * E
                    m = min(WARM, 512 - lo)
                    mm = nc.tensor.matmul(bank[0:T, lo:lo + m], x2T[:, n % 2, q], gateT[:, 0:m],
                                          start=True, stop=True)
                mm.then_inc(logits_mm, 1)

            pe.wait_ge(ident_ok, 1)
            pe.wait_ge(pool_const, 2)
            x_transposes(0, 0, 0)
            pe.wait_ge(wsplit, 2)
            gates(0, 0, True)
            x_transposes(1, 1, 0)
            pe.wait_ge(ab_in, 96)
            for n in range(2):
                nc.tensor.transpose(PW[0:ORDER, n * 128:(n + 1) * 128], ab[:, n], ident[:])
            mm = nc.tensor.transpose(PW[:, 256:256 + E], gate_in[:], ident[0:E, 0:E])
            mm.then_inc(filt_mm, 1)
            pe.wait_ge(filt_ev, 1)
            for n, which in enumerate((1, 1, 0, 0)):
                mm = nc.tensor.matmul(PW[0:NF, n * 128:(n + 1) * 128], dft_sb[:, n * NF:(n + 1) * NF],
                                      abT[:, which], start=True, stop=True)
            mm.then_inc(filt_mm, 1)
            x_transposes(2, 2, 0)
            gates(1, 1, False)
            pe.wait_ge(filt_step, FILT_LAST - 1)
            nc.tensor.matmul(PW[:, 0:T], fr[:, 10], idft_sb[:, 0:T], start=True, stop=False)
            nc.tensor.matmul(PW[:, 0:T], fr[:, 11], idft_sb[:, T:2 * T], start=False, stop=True).then_inc(filt_mm, 1)
            h_transposes(0, 0, True, False)
            pe.wait_ge(filt_step, FILT_LAST)
            w1_transposes(0, 0, 0, True)
            for c in range(2, 4):
                x_transposes(c + 1, (c + 1) % XBUF, (c + 1) // XBUF)
                gates(c, c % 2, False)
                h_transposes(c - 1, (c - 1) % 2, False, c == 2)
                w1_transposes(c - 1, (c - 1) % 2, (c - 1) // 2, False)
            with pe.Fori(1, NCH // 4 - 1) as i:
                for k in range(4):
                    c = i * 4 + k
                    x_transposes(c + 1, (k + 1) % XBUF, i + (k + 1) // XBUF)
                    gates(c, k % 2, False)
                    h_transposes(c - 1, (k + 1) % 2, False, False)
                    w1_transposes(c - 1, (k + 1) % 2, i * 2 + (k + 1) // 2 - 1, False)
            for c in range(NCH - 4, NCH):
                if c + 1 < NCH:
                    x_transposes(c + 1, (c + 1) % XBUF, (c + 1) // XBUF)
                gates(c, c % 2, False)
                h_transposes(c - 1, (c - 1) % 2, False, False)
                w1_transposes(c - 1, (c - 1) % 2, (c - 1) // 2, False)
            h_transposes(NCH - 1, (NCH - 1) % 2, False, False)
            w1_transposes(NCH - 1, (NCH - 1) % 2, (NCH - 1) // 2, False)
            pe.wait_ge(xn1_ready, NCH)
            for g in range(NCG):
                pe.wait_ge(hank_in[g * CG // HP], 16)
                if g >= 3:
                    pe.wait_ge(gelu_done, g - 2)
                for j in range(CG):
                    c = g * CG + j
                    n = WARM if j < CG - 1 else B
                    mm = nc.tensor.matmul(PG[g % 3][0:T, j * B:j * B + n], hank[0:T, c // HP % HRES, c % HP],
                                          XF[0:T, c * B:c * B + n], start=True, stop=True)
                mm.then_inc(conv_mm, 1)

            for n in range(2 * NHB):
                pe.wait_ge(xn2_ready, n // 2 + 1)
                pe.wait_ge(xn2_act, n // 2 + 1)
                if n >= 2:
                    pe.wait_ge(x2T_ready, n - 1)
                for q in range(4):
                    mm = nc.tensor.transpose(PR[n % 2][:, q * T:(q + 1) * T], XN[0:T, 4 * n + q], ident[0:T, 0:T])
                mm.then_inc(x2_transposed, 1)
                if n >= 1:
                    logits(n - 1)
            logits(2 * NHB - 1)

            pe.wait_ge(mask_ready, 1)
            for h in range(2):
                mm = nc.tensor.matmul(P[2 + h][0:128, :], oneb[0:T, :], maskb[0:T, h * 512:(h + 1) * 512],
                                      start=True, stop=True)
                mm.then_inc(prefix_mm, 1)
            for h in range(2):
                mm = nc.tensor.matmul(P[h][0:T, :], trib[0:T, 0:T], maskb[0:T, h * 512:(h + 1) * 512], start=True, stop=True)
            mm.then_inc(prefix_mm, 1)
            pe.wait_ge(ends_ready, 1)
            nc.tensor.matmul(P[5][0:1, 0:NT], onef[0:E - 1, 0:1], ends[:], start=True, stop=True).then_inc(eid_mm, 1)

            for n in range(2 * B):
                pe.wait_ge(onehot, n + 1)
                if n % OBUF in ON_ACT:
                    pe.wait_ge(onehot_act, share(n, ON_ACT) + 1)
                if n % OBUF in ON_POOL:
                    pe.wait_ge(onehot_pool, share(n, ON_POOL) + 1)
                mm = nc.tensor.matmul(P[4][:, 0:NT], ohl[0:T, n % OBUF], ohh[0:T, n % OBUF, 0:NT], start=(n == 0), stop=(n == 2 * B - 1))
                mm.then_inc(code_mm, 1)

            def g_transpose(n, k, nth):
                pe.wait_ge(gathered[k], 16 * (nth + 1))
                if not (isinstance(n, int) and n < 2):
                    pe.wait_ge(GT_ready, n - 1)
                nc.tensor.transpose(P[4 + k % 2][:, 0:SLOT], G[:, k], ident[:]).then_inc(g_transposed, 1)

            regs = [pe.alloc_register(f"pe_expert{k}") for k in range(UNROLL)]

            def experts_of(n):
                pe.load(regs, eid[0:1, bass.ds(n, UNROLL)])

            def expert(n, k, reg, first):
                e = pe.snap(regs[reg], min_val=0, max_val=E - 1)
                pe.wait_ge(GT_ready, n + 1)
                if not first:
                    pe.wait_ge(silu_done, n - 3)
                nc.tensor.matmul(P[k % 4][:, :], GT[:, k % 2], w1T[:, bass.ds(e * FF, FF)],
                                 start=True, stop=True).then_inc(expert_mm, 1)

            pe.wait_ge(eid_ready, 1)
            experts_of(0)
            g_transpose(0, 0, 0)
            for n in range(1, UNROLL + 1):
                g_transpose(n, n % GBUF, n // GBUF)
                expert(n - 1, n - 1, n - 1, n - 1 < 4)
            pe.wait_ge(R_ready, 1)
            for g in range(NHB):
                if g >= 2:
                    pe.wait_ge(tail_ev, g - 1)
                mm = nc.tensor.transpose(P[6 + g % 2][:, 0:T], L[0:T, g * HB:(g + 1) * HB].rearrange("p b e -> p (b e)"),
                                         ident[0:T, 0:T])
                mm.then_inc(tail_mm, 1)
            with pe.Fori(1, NT // UNROLL) as i:
                experts_of(i * UNROLL)
                for k in range(UNROLL - 1):
                    g_transpose(i * UNROLL + (k + 1), (k + 1) % GBUF, i * (UNROLL // GBUF) + (k + 1) // GBUF)
                    expert(i * UNROLL + k, k, k, False)
                g_transpose(i * UNROLL + UNROLL, 0, i * (UNROLL // GBUF) + UNROLL // GBUF)
                expert(i * UNROLL + (UNROLL - 1), UNROLL - 1, UNROLL - 1, False)
            rest = NT // UNROLL * UNROLL
            pe.load(regs[0:NT - rest], eid[0:1, rest:NT])
            for n in range(rest, NT):
                if n + 1 < NT:
                    g_transpose(n + 1, (n + 1) % GBUF, (n + 1) // GBUF)
                expert(n, n % UNROLL, n - rest, False)

            pe.wait_ge(esum_step, NT)
            for e in range(E):
                if e >= 4:
                    pe.wait_ge(y_step, e - 3)
                nc.tensor.matmul(P[e % 4][:, :], onef[:], esum[:, e * FF:(e + 1) * FF],
                                 start=True, stop=True).then_inc(hsum_mm, 1)
            pe.wait_ge(y_step, E + 1)
            nc.tensor.transpose(P[4][0:E, 0:128], y[:, 1, :], ident[:]).then_inc(tail_mm, 1)
            pe.wait_ge(tail_ev, NHB + 1)
            nc.tensor.matmul(P[5][:, 0:128], rep[:], yT[:], start=True, stop=True).then_inc(tail_mm, 1)
            nc.tensor.matmul(P[6][:, 0:128], rep[:], yT[:], start=True, stop=True).then_inc(tail_mm, 1)
            pe.wait_ge(tail_ev, NHB + 2)
            pe.wait_ge(ybd_dve, 1)
            yv = ybd[:].rearrange("p b d -> p (b d)")
            for n in range(2 * NHB):
                if n >= 4:
                    pe.wait_ge(mixed, n - 3)
                nc.tensor.matmul(P[n % 4][0:T, :], RT[:, n // 2, 0:T], yv[:, (n % 2) * 512:(n % 2 + 1) * 512],
                                 start=True, stop=True).then_inc(mix_mm, 1)

        @block.scalar
        def _(act):
            def gate_acts(c, k, first):
                for g, (dst, func) in enumerate(((zg, ACT.Tanh), (fg, ACT.Sigmoid), (og, ACT.Sigmoid))):
                    act.wait_ge(gate_mm, 3 * c + g + 1)
                    if not first and g == 0:
                        act.wait_ge(h_ready, c - 1)
                        act.wait_ge(hR_ready, c - 1)
                    src = PG[g][:, 0:XW].rearrange("p (b t) -> p b t", b=CB)[:, :, 0:T]
                    nc.scalar.activation(dst[:, k].rearrange("p (b t) -> p b t", b=CB), src, func).then_inc(gate_act, 1)

            def copy_xT(c, k, first):
                act.wait_ge(x_transposed, c + 1)
                if not first:
                    act.wait_ge(gate_mm, 3 * c - 3)
                nc.scalar.copy(xh[:, k], PX[:, 0:XW]).then_inc(xh_ready, 1)

            def copy_H(c):
                act.wait_ge(h_transposed, c + 1)
                nc.scalar.copy(H[0:T, bass.ds(c * CB, CB)].rearrange("p b c -> p (b c)") if not isinstance(c, int)
                               else H[0:T, c * CB:(c + 1) * CB].rearrange("p b c -> p (b c)"),
                               PH[0:T, :]).then_inc(H_ready, 1)

            def copy_w1T(e):
                act.wait_ge(w1_transposed, e + 1)
                nc.scalar.copy(w1T[:, bass.ds(e * FF, FF)] if not isinstance(e, int) else w1T[:, e * FF:(e + 1) * FF],
                               PW[:, :]).then_inc(w1T_ready, 1)

            copy_xT(0, 0, True)
            gate_acts(0, 0, True)
            copy_xT(1, 1, True)
            act.wait_ge(filt_mm, 1)
            act.wait_ge(pool_const, 1)
            nc.scalar.copy(gateT[:, 0:E], PW[:, 256:256 + E])
            nc.scalar.copy(abT[:].rearrange("p a c -> p (a c)"), PW[0:ORDER, 0:256]).then_inc(filt_ev, 1)
            copy_xT(2, 0, False)
            gate_acts(1, 1, True)
            copy_H(0)
            copy_w1T(0)
            act.wait_ge(filt_step, FILT_LAST)
            act.dma_start(kpad, kp[:]).then_inc(kpad_out, 16)
            for c in range(2, 4):
                copy_xT(c + 1, (c + 1) % 2, False)
                gate_acts(c, c % 2, False)
                copy_H(c - 1)
                copy_w1T(c - 1)
            with act.Fori(1, NCH // 4 - 1) as i:
                for k in range(4):
                    c = i * 4 + k
                    copy_xT(c + 1, (k + 1) % 2, False)
                    gate_acts(c, k % 2, False)
                    copy_H(c - 1)
                    copy_w1T(c - 1)
            for c in range(NCH - 4, NCH):
                if c + 1 < NCH:
                    copy_xT(c + 1, (c + 1) % 2, False)
                gate_acts(c, c % 2, False)
                copy_H(c - 1)
                copy_w1T(c - 1)
            copy_H(NCH - 1)
            copy_w1T(NCH - 1)

            for g in range(NCG):
                act.wait_ge(conv_mm, g + 1)
                if g >= 2:
                    act.wait_ge(H_added, g - 1)
                nc.scalar.activation(gl[0:T, g % 2].rearrange("p c b -> p (c b)"), PG[g % 3][0:T, :],
                                     ACT.Gelu_apprx_tanh).then_inc(gelu_done, 1)

            for n in range(2 * NHB):
                if n % 2 == 0:
                    g = n // 2
                    act.wait_ge(nmr_ready, g + 1)
                    for q in range(ACT_NORM, HB):
                        a = nc.scalar.activation(XN[0:T, g * HB + q], H[0:T, g * HB + q], ACT.Identity,
                                                 bias=nmr[0:T, g % 2, q:q + 1], scale=rs2[0:T, g % 2, q:q + 1])
                    a.then_inc(xn2_act, 1)
                act.wait_ge(x2_transposed, n + 1)
                if n >= 2:
                    act.wait_ge(logits_mm, n - 1)
                nc.scalar.copy(x2T[:, n % 2].rearrange("p b t -> p (b t)"), PR[n % 2][:, 0:4 * T]).then_inc(x2T_ready, 1)
            for h in range(2):
                act.wait_ge(logits_mm, (h + 1) * NHB)
                nc.scalar.copy(L[0:T, h * 32:(h + 1) * 32].rearrange("p b e -> p (b e)"), P[h][0:T, :]).then_inc(L_ready, 1)

            act.wait_ge(diff_ready, 1)
            nc.scalar.activation(wgt[0:T, 1], wgt[0:T, 0], ACT.Sigmoid)
            nc.scalar.activation(wgt[0:T, 2], wgt[0:T, 0], ACT.Sigmoid, scale=-1.0).then_inc(wgt_ready, 1)
            act.wait_ge(hilo_ready, 1)
            for n in range(2 * B):
                if n % OBUF in ON_ACT:
                    m = share(n, ON_ACT)
                    if m >= 2:
                        act.wait_ge(onehot_act, m - 1)
                    nc.scalar.activation(ohq[0:T, m % 2], iotb[0:T, 0:128], ACT.Square,
                                         bias=nlo[0:T, n:n + 1]).then_inc(act_square, 1)
                    if n >= OBUF:
                        act.wait_ge(code_mm, n - OBUF + 1)
                    act.wait_ge(act_square, m + 1)
                    nc.scalar.activation(ohl[0:T, n % OBUF], ohq[0:T, m % 2], ACT.Relu, bias=1.0,
                                         scale=-1.0).then_inc(onehot_act, 1)
            def copy_GT(n, k, first):
                act.wait_ge(g_transposed, n + 1)
                if not first:
                    act.wait_ge(expert_mm, n - 1)
                nc.scalar.copy(GT[:, k % 2], P[4 + k % 2][:, 0:SLOT]).then_inc(GT_ready, 1)

            def silu(n, k, first):
                act.wait_ge(expert_mm, n + 1)
                if not first:
                    act.wait_ge(esum_step, n - 3)
                nc.scalar.activation(S[:, k % 4], P[k % 4][:, :], ACT.Silu).then_inc(silu_done, 1)

            for n in range(UNROLL):
                copy_GT(n, n, n < 2)
                if n == 2:
                    act.wait_ge(R_ready, 1)
                if n >= 2:
                    silu(n - 2, n - 2, n - 2 < 4)
            for n in range(UNROLL, UNROLL + 1):
                copy_GT(n, n, False)
                silu(n - 2, n - 2, False)
                silu(n - 1, n - 1, False)
            for g in range(NHB):
                act.wait_ge(tail_mm, g + 1)
                nc.scalar.copy(RT[:, g, 0:T], P[6 + g % 2][:, 0:T]).then_inc(tail_ev, 1)
            with act.Fori(1, NT // UNROLL) as i:
                for k in range(UNROLL):
                    copy_GT(i * UNROLL + (k + 1), k + 1, False)
                    silu(i * UNROLL + k, k, False)
            for n in range(NT // UNROLL * UNROLL, NT):
                if n + 1 < NT:
                    copy_GT(n + 1, n + 1, False)
                silu(n, n % UNROLL, False)

            act.wait_ge(tail_mm, NHB + 1)
            nc.scalar.copy(yT[:], P[4][0:E, 0:128]).then_inc(tail_ev, 1)
            act.wait_ge(tail_mm, NHB + 2)
            for b in range(HB // 2):
                a = nc.scalar.mul(ybd[:, b], P[5][:, 0:128], bmask[:, b:b + 1])
            a.then_inc(tail_ev, 1)

        @block.vector
        def _(dve):
            v = nc.vector

            def moments(st, m, ve, done, count, ready):
                v.tensor_tensor(m[:, 1], st[:, :, 1], st[:, :, 4], ALU.subtract)
                v.tensor_tensor(m[:, 2], st[:, :, 2], st[:, :, 5], ALU.add)
                v.tensor_tensor(m[:, 0], st[:, :, 1], st[:, :, 4], ALU.add).then_inc(done, 1)
                dve.wait_ge(done, count + 1)
                v.scalar_tensor_tensor(out=m[:, 1], in0=m[:, 1], scalar=0.25, in1=m[:, 1],
                                       op0=ALU.mult, op1=ALU.mult)
                v.tensor_scalar(m[:, 2], m[:, 2], 1.0 / D, EPS, ALU.mult, ALU.add).then_inc(done, 1)
                dve.wait_ge(done, count + 2)
                v.tensor_scalar(m[:, 0], m[:, 0], 0.5, None, ALU.mult).then_inc(done, 1)
                v.tensor_tensor(ve, m[:, 1], m[:, 2], ALU.add).then_inc(ready, 1)

            def cell(c, k):
                dve.wait_ge(gate_act, 3 * c + 3)
                if not (isinstance(c, int) and c < 2):
                    dve.wait_ge(hR_ready, c - 1)
                v.scalar_tensor_tensor(out=cc[:, k], in0=fg[:, k], scalar=-1.0, in1=zg[:, k],
                                       op0=ALU.add, op1=ALU.mult).then_inc(cell_step, 1)
                dve.wait_ge(cell_step, 3 * c + 1)
                v.memset(fg[:, k].rearrange("p (b t) -> p b t", b=CB)[:, :, 0:1], 0.0).then_inc(cell_step, 1)
                dve.wait_ge(cell_step, 3 * c + 2)
                v.tensor_tensor_scan(cc[:, k], fg[:, k], cc[:, k], 0.0, ALU.mult, ALU.subtract).then_inc(cell_step, 1)
                dve.wait_ge(cell_step, 3 * c + 3)
                if not (isinstance(c, int) and c < 2):
                    dve.wait_ge(h_transposed, c - 1)
                v.tensor_tensor(hT[:, k], cc[:, k], og[:, k], ALU.mult).then_inc(h_ready, 1)

            def stats(c, k):
                dve.wait_ge(h_transposed, c + 1)
                for q in range(CB):
                    a = v.bn_stats(st1[0:T, k, q], PR[k][0:T, q * D:(q + 1) * D])
                a.then_inc(bn1, 1)
                dve.wait_ge(bn1, 4 * c + 1)
                moments(st1[0:T, k], mm1[0:T, k], ve1[0:T, k], bn1, 4 * c + 1, ve1_ready)

            def norm(c, k):
                dve.wait_ge(rstd1, c + 1)
                for q in range(CB):
                    at = c * CB + q
                    dst = XC[0:T, :, at] if isinstance(at, int) else XC[0:T, :, bass.ds(at, 1)].rearrange("p c a -> p (c a)")
                    a = v.tensor_scalar(dst, PR[k][0:T, q * D:(q + 1) * D], mm1[0:T, k, 0, q:q + 1], rs1[0:T, k, q:q + 1],
                                        ALU.subtract, ALU.mult)
                a.then_inc(xn1_ready, 1)

            def low_part(c, k):
                dve.wait_ge(xh_ready, c + 1)
                v.tensor_tensor(xl[:, k], PX[:, 0:XW], xh[:, k].bitcast(FP32), ALU.subtract).then_inc(xl_ready, 1)

            dve.wait_ge(wk_in, 16)
            v.tensor_copy(wh[:], wk[:]).then_inc(wsplit, 1)
            dve.wait_ge(wsplit, 1)
            v.tensor_tensor(wl[:], wk[:], wh[:].bitcast(FP32), ALU.subtract).then_inc(wsplit, 1)
            low_part(0, 0)
            cell(0, 0)
            low_part(1, 1)
            low_part(2, 0)
            steps = [0]

            def fstep(ins):
                steps[0] += 1
                ins.then_inc(filt_step, 1)
                dve.wait_ge(filt_step, steps[0])

            dve.wait_ge(filt_mm, 2)
            fstep(v.tensor_copy(fr[:, 0:4].rearrange("p a c -> p (a c)"), PW[0:NF, :]))
            fstep(v.tensor_scalar(fr[:, 2], fr[:, 2], 1.0, None, ALU.add))
            fstep(v.tensor_tensor(fr[:, 4:6], fr[:, 2:4], fr[:, 2:4], ALU.mult))
            fstep(v.tensor_tensor(fr[:, 6], fr[:, 4], fr[:, 5], ALU.add))
            fstep(v.reciprocal(fr[:, 7], fr[:, 6]))
            v.tensor_tensor(fr[:, 4], fr[:, 0], fr[:, 2], ALU.mult)
            v.tensor_tensor(fr[:, 5], fr[:, 1], fr[:, 3], ALU.mult)
            v.tensor_tensor(fr[:, 8], fr[:, 1], fr[:, 2], ALU.mult)
            fstep(v.tensor_tensor(fr[:, 9], fr[:, 0], fr[:, 3], ALU.mult))
            fstep(v.tensor_tensor(fr[:, 4], fr[:, 4], fr[:, 5], ALU.add))
            fstep(v.tensor_tensor(fr[:, 8], fr[:, 8], fr[:, 9], ALU.subtract))
            fstep(v.tensor_tensor(fr[:, 10], fr[:, 4], fr[:, 7], ALU.mult))
            fstep(v.tensor_tensor(fr[:, 11], fr[:, 8], fr[:, 7], ALU.mult))
            steps[0] += 1
            v.tensor_copy(fr[:, 6], fr[:, 7]).then_inc(filt_step, 1)
            dve.wait_ge(filt_step, steps[0])
            cell(1, 1)
            dve.wait_ge(filt_mm, 3)
            dve.wait_ge(pool_const, 1)
            dve.wait_ge(ab_in, 96)
            v.tensor_copy(kp[:, T:2 * T - 1], PW[:, 1:T])
            v.tensor_scalar(kp[:, T - 1:T], PW[:, 0:1], h0c[:, 0:1], None, ALU.add).then_inc(filt_step, 1)
            assert steps[0] + 1 == FILT_LAST, steps[0]
            stats(0, 0)
            for c in range(2, 4):
                low_part(c + 1, (c + 1) % 2)
                cell(c, c % 2)
                stats(c - 1, (c - 1) % 2)
                norm(c - 2, c % 2)
            with dve.Fori(1, NCH // 4 - 1) as i:
                for k in range(4):
                    c = i * 4 + k
                    low_part(c + 1, (k + 1) % 2)
                    cell(c, k % 2)
                    stats(c - 1, (k + 1) % 2)
                    norm(c - 2, k % 2)
            for c in range(NCH - 4, NCH):
                if c + 1 < NCH:
                    low_part(c + 1, (c + 1) % 2)
                cell(c, c % 2)
                stats(c - 1, (c - 1) % 2)
                norm(c - 2, c % 2)
            stats(NCH - 1, (NCH - 1) % 2)
            norm(NCH - 2, NCH % 2)
            norm(NCH - 1, (NCH - 1) % 2)

            dve.wait_ge(H_ready, NCH)
            with dve.Fori(0, NCG // 2) as i:
                for k in range(2):
                    g = i * 2 + k
                    dve.wait_ge(gelu_done, g + 1)
                    hv = H[0:T, :, bass.ds(g * CG, CG)].rearrange("p b c -> p c b")
                    v.tensor_tensor(hv, hv, gl[0:T, k], ALU.add).then_inc(H_added, 1)
            dve.wait_ge(H_added, NCG)

            def norm2(g):
                dve.wait_ge(rstd2, g + 1)
                if g >= 2:
                    dve.wait_ge(xn2_act, g - 1)
                v.scalar_tensor_tensor(out=nmr[0:T, g % 2], in0=mm2[0:T, g % 2, 0], scalar=-1.0, in1=rs2[0:T, g % 2],
                                       op0=ALU.mult, op1=ALU.mult).then_inc(nmr_ready, 1)
                for q in range(ACT_NORM):
                    b = g * HB + q
                    a = v.tensor_scalar(XN[0:T, b], H[0:T, b], mm2[0:T, g % 2, 0, q:q + 1], rs2[0:T, g % 2, q:q + 1],
                                        ALU.subtract, ALU.mult)
                a.then_inc(xn2_ready, 1)

            for g in range(NHB):
                for q in range(HB):
                    a = v.bn_stats(st2[0:T, g % 2, q], H[0:T, g * HB + q])
                a.then_inc(bn2, 1)
                dve.wait_ge(bn2, 4 * g + 1)
                moments(st2[0:T, g % 2], mm2[0:T, g % 2], ve2[0:T, g % 2], bn2, 4 * g + 1, ve2_ready)
                if g >= 1:
                    norm2(g - 1)
            norm2(NHB - 1)

            rs = [0]

            def step(ins):
                rs[0] += 1
                ins.then_inc(route_step, 1)
                dve.wait_ge(route_step, rs[0])

            dve.wait_ge(pool_const, 2)
            dve.wait_ge(L_ready, 2)
            dve.wait_ge(const_in, 32)

            def per_b(n):
                return mx[0:T, n].unsqueeze(2).to_broadcast([T, B, E])

            rk = rank_sb[0:T].unsqueeze(1).to_broadcast([T, B, E])
            src = L
            for k in range(2):
                step(v.tensor_reduce(mx[0:T, k], src[0:T], AX.X, ALU.max))
                step(v.tensor_tensor(OH[k][0:T], src[0:T], per_b(k), ALU.is_equal))
                step(v.tensor_tensor(OH[k][0:T], OH[k][0:T], rk, ALU.mult))
                step(v.tensor_reduce(mx[0:T, 2 + k], OH[k][0:T], AX.X, ALU.max))
                step(v.tensor_tensor(OH[k][0:T], rk, per_b(2 + k), ALU.is_equal))
                if k == 0:
                    step(v.scalar_tensor_tensor(out=LW[0:T], in0=OH[0][0:T], scalar=NEG, in1=L[0:T],
                                                op0=ALU.mult, op1=ALU.add))
                    src = LW
            v.tensor_tensor(wgt[0:T, 0], mx[0:T, 0], mx[0:T, 1], ALU.subtract).then_inc(diff_ready, 1)
            v.tensor_tensor(maskb[0:T].rearrange("p (b e) -> p b e", b=B), OH[0][0:T], OH[1][0:T],
                            ALU.add).then_inc(mask_ready, 1)
            for h in range(2):
                dve.wait_ge(prefix_mm, h + 1)
                a = v.tensor_copy(tot[:, :, h * 32:(h + 1) * 32],
                                  P[2 + h][:, :].rearrange("p (b e) -> p e b", b=32))
            step(a)
            flat = tot.rearrange("p e b -> p (e b)")
            step(v.tensor_tensor_scan(cum.rearrange("p e b -> p (e b)"), flat, flat, 0.0, ALU.add, ALU.max))
            step(v.tensor_copy(small[:, 0], cum[:, :, B - 1]))
            v.tensor_copy(small[:, 1, 0:1], small[:, 0, 0:1])
            step(v.tensor_tensor(small[:, 1, 1:E], small[:, 0, 1:E], small[:, 0, 0:E - 1], ALU.subtract))
            step(v.tensor_scalar(smi[:, 0], small[:, 1], float(SLOT - 1), None, ALU.add))
            step(v.tensor_scalar(smi[:, 1], smi[:, 0], 7, None, ALU.arith_shift_right))
            step(v.tensor_copy(small[:, 4], smi[:, 1]))
            step(v.tensor_tensor_scan(small[:, 2], small[:, 4], small[:, 4], 0.0, ALU.add, ALU.max))
            v.tensor_scalar(small[:, 3, 0:1], small[:, 0, 0:1], 0.0, None, ALU.mult)
            step(v.scalar_tensor_tensor(out=small[:, 3, 1:E], in0=small[:, 2, 0:E - 1], scalar=float(SLOT),
                                        in1=small[:, 0, 0:E - 1], op0=ALU.mult, op1=ALU.subtract))
            step(v.tensor_tensor(cum[:], cum[:], tot[:], ALU.subtract))
            step(v.tensor_tensor(cum[:], cum[:], small[:, 3].unsqueeze(2).to_broadcast([128, E, B]), ALU.add))
            step(v.tensor_tensor(y[0:E, 0], small[0:E, 2], ident[0:E, 0:E], ALU.mult))
            step(v.tensor_reduce(small[0:E, 4, 0:1], y[0:E, 0], AX.X, ALU.add))
            v.tensor_scalar(ends[:], iotb[0:E - 1, :], small[0:E - 1, 4, 0:1], None, ALU.is_ge).then_inc(ends_ready, 1)
            dve.wait_ge(prefix_mm, 3)
            for h in range(2):
                a = v.tensor_tensor(LW[0:T, h * 32:(h + 1) * 32],
                                    P[h][0:T, :].rearrange("p (b e) -> p b e", b=32),
                                    cum[0:T, :, h * 32:(h + 1) * 32].rearrange("p e b -> p b e"), ALU.add)
            step(a)
            for k in range(2):
                step(v.tensor_tensor(tot[0:T].rearrange("p e b -> p (e b)").rearrange("p (b e) -> p b e", b=B),
                                     LW[0:T], OH[k][0:T], ALU.mult))
                step(v.tensor_reduce(pos[0:T, k * B:(k + 1) * B],
                                     tot[0:T].rearrange("p e b -> p (e b)").rearrange("p (b e) -> p b e", b=B),
                                     AX.X, ALU.add))
            step(v.tensor_copy(posi[0:T, 0], pos[0:T]))
            v.tensor_scalar(posi[0:T, 1], posi[0:T, 0], 7, None, ALU.arith_shift_right)
            step(v.tensor_scalar(posi[0:T, 2], posi[0:T, 0], SLOT - 1, None, ALU.bitwise_and))
            v.tensor_scalar(nlo[0:T], posi[0:T, 2], -1.0, None, ALU.mult)
            v.tensor_copy(hilo[0:T], posi[0:T, 1:3]).then_inc(hilo_ready, 1)
            dve.wait_ge(hilo_ready, 1)

            dve.wait_ge(eid_mm, 1)
            v.tensor_copy(eid[:], P[5][0:1, 0:NT]).then_inc(eid_ready, 1)

            for n in range(2 * B):
                if n >= OBUF:
                    dve.wait_ge(code_mm, n - OBUF + 1)
                if n % OBUF not in ON_ACT + ON_POOL:
                    v.tensor_scalar(ohl[0:T, n % OBUF], iotb[0:T, 0:128], hilo[0:T, 1, n:n + 1], None, ALU.is_equal)
                v.tensor_scalar(ohh[0:T, n % OBUF, 0:NT], iotb[0:T], hilo[0:T, 0, n:n + 1], code_sb[0:T, n % B:n % B + 1],
                                ALU.is_equal, ALU.mult).then_inc(onehot, 1)
            dve.wait_ge(code_mm, 2 * B)
            step(v.tensor_scalar(idx[:], P[4][:, 0:NT].bitcast(I32), 16, None, ALU.arith_shift_right))
            step(v.tensor_scalar(idx[:], idx[:], float((127 - EXPO - 1) * 128), 0.0, ALU.subtract, ALU.max))
            step(v.tensor_scalar(idx2[:], idx[:], 7, None, ALU.arith_shift_right))
            step(v.scalar_tensor_tensor(out=idx[:], in0=idx2[:], scalar=float(T - 128), in1=idx[:],
                                        op0=ALU.mult, op1=ALU.add))
            v.tensor_scalar(idx[:], idx[:], float(T - 1), 0.0, ALU.subtract, ALU.max).then_inc(idx_ready, 1)
            dve.wait_ge(wgt_ready, 1)
            for k in range(2):
                step(v.tensor_tensor(OH[k][0:T], OH[k][0:T],
                                     wgt[0:T, 1 + k].unsqueeze(2).to_broadcast([T, B, E]), ALU.mult))
            v.tensor_tensor(L[0:T], OH[0][0:T], OH[1][0:T], ALU.add).then_inc(R_ready, 1)
            step(v.tensor_scalar(small[:, 5], small[:, 1], 1.0, None, ALU.max))
            step(v.reciprocal(small[:, 6], small[:, 5]))

            dve.wait_ge(esum_clear, NHB)
            dve.wait_ge(eid_ready, 1)

            regs = [dve.alloc_register(f"dve_expert{k}") for k in range(UNROLL)]

            def accumulate(n, k, reg, first):
                e = dve.snap(regs[reg], min_val=0, max_val=E - 1)
                dve.wait_ge(silu_done, n + 1)
                if not first:
                    dve.wait_ge(esum_step, n)
                at = esum[:, bass.ds(e * FF, FF)]
                v.tensor_tensor(at, at, S[:, k % 4], ALU.add).then_inc(esum_step, 1)

            dve.load(regs, eid[0:1, 0:UNROLL])
            for n in range(UNROLL):
                accumulate(n, n, n, n == 0)
            with dve.Fori(1, NT // UNROLL) as i:
                dve.load(regs, eid[0:1, bass.ds(i * UNROLL, UNROLL)])
                for k in range(UNROLL):
                    accumulate(i * UNROLL + k, k, k, False)
            rest = NT // UNROLL * UNROLL
            dve.load(regs[0:NT - rest], eid[0:1, rest:NT])
            for n in range(rest, NT):
                accumulate(n, n, n - rest, False)

            dve.wait_ge(w2_in, 16)
            for e in range(E):
                dve.wait_ge(hsum_mm, e + 1)
                if e >= 1:
                    dve.wait_ge(y_step, e)
                v.tensor_tensor_reduce(out=junk[:], in0=w2_sb[:, e], in1=P[e % 4][:, :], scale=1.0, scalar=0.0,
                                       op0=ALU.mult, op1=ALU.add, accum_out=y[:, 0, e:e + 1]).then_inc(y_step, 1)
            dve.wait_ge(y_step, E)
            v.tensor_tensor(y[:, 1], y[:, 0], small[:, 6], ALU.mult).then_inc(y_step, 1)
            dve.wait_ge(tail_mm, NHB + 3)
            for b in range(HB // 2, HB):
                a = v.tensor_scalar(ybd[:, b], P[6][:, 0:128], bmask[:, b:b + 1], None, ALU.mult)
            a.then_inc(ybd_dve, 1)
            for n in range(2 * NHB):
                dve.wait_ge(mix_mm, n + 1)
                hv = H[0:T, 4 * n:4 * (n + 1)].rearrange("p b c -> p (b c)")
                v.tensor_tensor(hv, P[n % 4][0:T, :], hv, ALU.add).then_inc(mixed, 1)


_INS = ["x", "L0_tok_kernel", "L0_attn_A", "L0_attn_B", "L0_attn_h0", "L0_ffn_gate_weight", "L0_ffn_w1", "L0_ffn_w2"]


def kernel(**inputs):
    import numpy as _np
    import concourse.bacc as _bacc
    from concourse import mybir as _mybir
    from concourse.bass_utils import run_bass_kernel_spmd as _run

    nc = _bacc.Bacc("TRN2", target_bir_lowering=False, num_devices=1)
    arrays, args = {}, []
    for name in _INS:
        arrays[f"in_{name}"] = _np.ascontiguousarray(inputs[name])
    for name, a in tables().items():
        arrays[f"const_{name}"] = a
    for name, a in arrays.items():
        args.append(nc.dram_tensor(name, a.shape, _mybir.dt.from_np(a.dtype), kind="ExternalInput").ap())
    args.append(nc.dram_tensor("out", (B, T, D), FP32, kind="ExternalOutput").ap())
    args.append(nc.dram_tensor("kpad", (D, KROW), FP32, kind="Internal").ap())
    args.append(nc.dram_tensor("table", (NTOK + 1, D), FP32, kind="Internal").ap())
    build(nc, *args)
    return _run(nc, [arrays], core_ids=[0]).results[0]["out"]
```

```python
from contextlib import ExitStack

import numpy as np

import concourse.bass as bass
from concourse import mybir

FP32 = mybir.dt.float32
FP32R = mybir.dt.float32r
BF16 = mybir.dt.bfloat16
I32 = mybir.dt.int32
ALU = mybir.AluOpType
ACT = mybir.ActivationFunctionType
AX = mybir.AxisListType

B, TIN, D = 64, 125, 128
WIN = 3
T = TIN - WIN + 1
ORDER = 64
NF = T // 2 + 1
E, FF = 16, 512
EPS = 1e-5

CB = 4
NCH = B // CB
CW = CB * T
XW = CB * TIN
NV = XW - WIN + 1
XBUF = 4

CG = 8
NCG = D // CG
HP = 8
NHP = D // HP
HRES = 12
HLAG = 4
KROW = 256
WARM = 112
HB = 8
NHB = B // HB
NORM_DVE, NORM_POOL = 2, 1
NORM_DVE_LAST = 4

SLOT = 128
NTOK = B * T
NT = (2 * NTOK + E * (SLOT - 1)) // SLOT
UNROLL = 12
GBUF = 6
OG = 4
OBUF = 16
ON_POOL = 1
assert NT % GBUF == 0 and NT <= 256
SPLIT = 112

EXPO = 32
TROW = 128
NEG = -3.0e38
ARENA = 10128


def tables():
    n = np.arange(ORDER, dtype=np.float64)[:, None]
    k = np.arange(NF, dtype=np.float64)[None, :]
    w = 2 * np.pi * k / T
    m = np.arange(T, dtype=np.float64)[None, :]
    half = np.where(np.arange(NF) == 0, 1.0, 2.0)[:, None] / T
    ph = 2 * np.pi * k.T * (T - 1 - m) / T
    out = {
        "dft": np.concatenate([np.cos(w * n), -np.sin(w * n), np.cos(w * (n + 1)), -np.sin(w * (n + 1))], 1),
        "idft": np.concatenate([half * np.cos(ph), -half * np.sin(ph)], 1),
        "code": (1 + np.arange(128)[:, None] / 128.0) * 2.0 ** (np.arange(B)[None, :] - EXPO),
        "rank": np.tile(E - np.arange(E)[None, :], (128, 1)),
    }
    return {k: v.astype(np.float32) for k, v in out.items()}


def build(nc, x, wconv, fa, fb, h0, gate, w1, w2, dft, idft, code, rank, out, kpad, table):
    ctx = ExitStack()

    def sb(name, shape, dt=FP32):
        return ctx.enter_context(nc.sbuf_tensor(name, shape, dt))

    def pb(name):
        return ctx.enter_context(nc.psum_tensor(name, [128, 512], FP32))

    def sem(name):
        return ctx.enter_context(nc.semaphore(name))

    with ctx:
        BIG = sb("BIG", [128, 3 * E * FF // 2])
        hank = BIG[:, 0:HRES * HP * T].rearrange("p (q c t) -> p q c t", q=HRES, c=HP)
        w1raw = BIG[:, 0:E * FF].rearrange("p (e q d) -> p e q d", e=E, q=4)
        esum = BIG[:, 0:E * FF]
        w1T = sb("w1T", [128, E * FF])
        H = sb("H", [128, B, D])
        XN = sb("XN", [128, B, D])
        XF = XN[:].rearrange("p b c -> p (b c)")
        XC = XN[:].rearrange("p b c -> p (b c)").rearrange("p (c b) -> p c b", c=D)
        w2_sb = XN[:].rearrange("p b c -> p (b c)").rearrange("p (e f) -> p e f", e=E)
        wh = sb("wh", [128, WIN, 3 * D], FP32R)
        wl = sb("wl", [128, WIN, 3 * D], FP32R)
        xh = sb("xh", [128, 2, XW], FP32R)
        xl = sb("xl", [128, 2, XW], FP32R)
        arena = sb("arena", [128, ARENA])
        used = [0]

        def carve(*dims, dt=FP32):
            n = int(np.prod(dims))
            words = n if dt != BF16 else (n + 1) // 2
            part = arena[:, used[0]:used[0] + words]
            used[0] += words
            assert used[0] <= ARENA, used[0]
            if dt != FP32:
                part = part.bitcast(dt)[:, 0:n]
            if len(dims) == 2:
                part = part.rearrange("p (a b) -> p a b", a=dims[0])
            if len(dims) == 3:
                part = part.rearrange("p (a b c) -> p a b c", a=dims[0], b=dims[1])
            return part

        wk = carve(WIN, 3 * D)
        xin = carve(XBUF, CB, D)
        zg = carve(2, CW)
        fg = carve(2, CW)
        og = carve(2, CW)
        cc = carve(2, CW)
        hT = carve(2, CW)
        stage = carve(2, HP * T).rearrange("p k (c t) -> p k c t", c=HP)
        used[0] = 0
        gl = carve(2, CG, B)
        x2T = carve(2, 4, T)
        L = carve(B, E)
        LW = carve(B, E)
        cum = carve(E, B)
        picked = carve(B, E)
        G = carve(GBUF, D)
        posi = carve(3, 2 * B, dt=I32)
        hilo = carve(2, 2 * B)
        GT = carve(2, SLOT)
        st2 = carve(2, HB * 6).rearrange("p a (q n) -> p a q n", q=HB)
        small = carve(7, E)
        y = carve(E)
        yrep = carve(HB, E)
        ohl = carve(OBUF, 128, dt=BF16)
        ohq = carve(3, OG * 128, dt=BF16)
        loT = carve(T, dt=BF16)
        minus1b = carve(128, dt=BF16)
        iota1b = carve(128, dt=BF16)
        at = E * FF
        S = BIG[:, at:at + 4 * FF].rearrange("p (k f) -> p k f", k=4)
        OH = BIG[:, at:at + B * E].bitcast(BF16).rearrange("p (k b e) -> p k b e", k=2, b=B)
        OH = [OH[:, 0], OH[:, 1]]
        at += 4 * FF
        maskb = BIG[:, at:at + B * E // 2].bitcast(BF16)
        at += B * E // 2
        ohh = BIG[:, at:at + OBUF * (NT // 2)].bitcast(BF16).rearrange("p (k n) -> p k n", k=OBUF)
        RTh, RTl = (a[:, :, 0:4 * T].rearrange("p h (g t) -> p h g t", g=4) for a in (xh, xl))
        yh, yl = (a[:].rearrange("p w n -> p (w n)")[:, 0:HB * D].rearrange("p (b d) -> p b d", b=HB) for a in (wh, wl))
        sumh, suml = (a[:].rearrange("p w n -> p (w n)")[:, 0:2 * FF].rearrange("p (k f) -> p k f", k=2) for a in (wh, wl))
        gl0 = gl[:, 0].rearrange("p c b -> p (c b)")
        gl1 = gl[:, 1].rearrange("p c b -> p (c b)")
        mx = gl0[:, 0:2 * B].rearrange("p (n b) -> p n b", n=2)
        pos = gl0[:, 2 * B:4 * B]
        wgt = gl1[:, 0:3 * B].rearrange("p (n b) -> p n b", n=3)
        idx = gl1[:, 3 * B:3 * B + NT].bitcast(I32)
        junk = (gl0, gl1)
        lw = LW.rearrange("p b e -> p (b e)")
        ends = gl1[0:E - 1, 3 * B + NT:3 * B + 2 * NT]
        eid = lw[0:1, 0:NT].bitcast(I32)

        st1 = sb("st1", [128, 2, CB, 6])
        mm1 = sb("mm1", [128, 2, 3, CB])
        ve1 = sb("ve1", [128, 2, CB])
        rs1 = sb("rs1", [128, 2, CB])
        mhalf = sb("mhalf", [128, HB])
        ident = sb("ident", [128, 128])
        fr = w1T[0:NF, 12 * FF:15 * FF].rearrange("p (a c) -> p a c", a=12)
        dft_sb = w1T[0:ORDER, 15 * FF:15 * FF + 4 * NF]
        idft_sb = w1T[0:NF, 15 * FF + 4 * NF:15 * FF + 4 * NF + 2 * T]
        ab = XN[:, B - 1].rearrange("p (a n) -> p a n", a=2)
        gate_in = XN[0:E, B - 4]
        kp = H[:, B - 2:B].rearrange("p a n -> p (a n)")
        abT = XN[0:ORDER, B - 3:B - 1]
        code_sb = sb("code_sb", [128, B])
        rank_sb = sb("rank_sb", [128, E])
        rankb = sb("rankb", [128, E], BF16)
        firstb = sb("firstb", [128, 2, B], BF16)
        h0c = sb("h0c", [128, 1])
        gateT = sb("gateT", [128, WARM])
        mm2 = sb("mm2", [128, 2, 3, HB])
        ve2 = sb("ve2", [128, 2, HB])
        rs2 = sb("rs2", [128, 2, HB])
        nmr = sb("nmr", [128, 2, HB])
        trib = sb("trib", [128, 128], BF16)
        oneb = sb("oneb", [128, 128], BF16)
        minusb = sb("minusb", [128, 128], BF16)
        smi = sb("smi", [128, 2, E], I32)
        iotb = sb("iotb", [128, NT], BF16)
        bmask = sb("bmask", [128, HB])
        onef = sb("onef", [128, 128])
        oner = sb("oner", [128, 128], FP32R)

        P = [pb(f"P{n}") for n in range(8)]
        PG, PX, PH, PR, PW = P[0:3], P[3], (P[4], P[5]), P[5:7], P[7]
        PD = (P[2], P[3], P[0])
        PT = (P[4], P[7])

        const_in = sem("const_in")
        wk_in = sem("wk_in")
        ab_in = sem("ab_in")
        x_in = [sem(f"x_in{n}") for n in range(XBUF)]
        w1_in = [sem(f"w1_in{n}") for n in range(2)]
        w2_in = sem("w2_in")
        kpad_out = sem("kpad_out")
        stage_in = [sem(f"stage_in{n}") for n in range(2)]
        hank_ready = sem("hank_ready")
        table_out = sem("table_out")
        zero_out = sem("zero_out")
        out_done = sem("out_done")
        pool_const = sem("pool_const")
        pool_step = sem("pool_step")
        ident_ok = sem("ident_ok")
        x_transposed = sem("x_transposed")
        xh_ready = sem("xh_ready")
        xl_ready = sem("xl_ready")
        wsplit = sem("wsplit")
        gate_mm = sem("gate_mm")
        gate_act = sem("gate_act")
        w1_transposed = sem("w1_transposed")
        w1T_ready = sem("w1T_ready")
        cell_step = sem("cell_step")
        h_ready = sem("h_ready")
        h_transposed = sem("h_transposed")
        H_ready = sem("H_ready")
        bn1 = sem("bn1")
        ve1_ready = sem("ve1_ready")
        rstd1 = sem("rstd1")
        xn1_ready = sem("xn1_ready")
        filt_mm = sem("filt_mm")
        filt_ev = sem("filt_ev")
        filt_step = sem("filt_step")
        conv_mm = sem("conv_mm")
        gelu_done = sem("gelu_done")
        H_added = sem("H_added")
        bn2 = sem("bn2")
        ve2_ready = sem("ve2_ready")
        rstd2 = sem("rstd2")
        xn2_ready = sem("xn2_ready")
        nmr_ready = sem("nmr_ready")
        xn2_act = sem("xn2_act")
        xn2_pool = sem("xn2_pool")
        LW_ready = sem("LW_ready")
        picked_pool = sem("picked_pool")
        x2_transposed = sem("x2_transposed")
        x2T_ready = sem("x2T_ready")
        logits_mm = sem("logits_mm")
        route_step = sem("route_step")
        mask_ready = sem("mask_ready")
        prefix_mm = sem("prefix_mm")
        diff_ready = sem("diff_ready")
        wgt_ready = sem("wgt_ready")
        hilo_ready = sem("hilo_ready")
        onehot = sem("onehot")
        onehot_act = sem("onehot_act")
        onehot_pool = sem("onehot_pool")
        act_square = sem("act_square")
        lo_mm = sem("lo_mm")
        loT_ready = sem("loT_ready")
        distance_mm = sem("distance_mm")
        L_ready = sem("L_ready")
        code_mm = sem("code_mm")
        idx_ready = sem("idx_ready")
        ends_ready = sem("ends_ready")
        eid_mm = sem("eid_mm")
        eid_ready = sem("eid_ready")
        esum_clear = sem("esum_clear")
        gathered = [sem(f"gathered{n}") for n in range(GBUF)]
        g_transposed = sem("g_transposed")
        GT_ready = sem("GT_ready")
        expert_mm = sem("expert_mm")
        silu_done = sem("silu_done")
        esum_step = sem("esum_step")
        hsum_mm = sem("hsum_mm")
        y_step = sem("y_step")
        R_ready = sem("R_ready")
        RT_mm = sem("RT_mm")
        RT_high = sem("RT_high")
        mix_mm = sem("mix_mm")
        mixed = sem("mixed")
        RT_low = sem("RT_low")
        sum_high = sem("sum_high")
        sum_low = sem("sum_low")
        y_transposed = sem("y_transposed")
        yh_ready = sem("yh_ready")
        yl_ready = sem("yl_ready")

        xr = x.rearrange("(n b) t d -> n t b d", b=CB)
        w1r = w1.rearrange("e (q p) d -> p e q d", p=128)
        FILT_LAST = 12
        W1_FIRST = 12
        RT_AT = (5, 10)

        def dve_norms(g):
            return NORM_DVE_LAST if g == NHB - 1 else NORM_DVE

        on_act = [j for j in range(2 * B // OG) if j % (OBUF // OG) != ON_POOL]

        def pool_made(n):
            return n // OG % (OBUF // OG) == ON_POOL

        in_parts = list(range(3, E, 2))

        def hankel(q):
            return bass.AP(kpad.tensor, q * HP * KROW, [[1, 128], [KROW, HP], [1, T]])

        block = ctx.enter_context(nc.Block())

        @block.sync
        def _(sp):
            sp.dma_start(xin[0:TIN, 0], xr[0]).then_inc(x_in[0], 16)
            sp.dma_start(wk[:], wconv.rearrange("w d n -> d w n")).then_inc(wk_in, 16)
            sp.dma_start(xin[0:TIN, 1], xr[1]).then_inc(x_in[1], 16)
            sp.dma_start(ab[:, 0], fa).then_inc(ab_in, 16)
            sp.dma_start(ab[:, 1], fb).then_inc(ab_in, 16)
            sp.dma_start(dft_sb[:], dft).then_inc(ab_in, 16)
            sp.dma_start(idft_sb[:], idft).then_inc(ab_in, 16)
            sp.dma_start(h0c[:], bass.AP(h0.tensor, 0, [[0, 128], [1, 1]])).then_inc(ab_in, 16)
            sp.dma_start(gate_in[:], gate).then_inc(ab_in, 16)
            for n in range(2, XBUF):
                sp.dma_start(xin[0:TIN, n], xr[n]).then_inc(x_in[n], 16)
            sp.dma_start(code_sb[:], code).then_inc(const_in, 16)
            sp.dma_start(rank_sb[:], rank).then_inc(const_in, 16)
            def load_piece(q):
                if q >= 2:
                    sp.wait_ge(hank_ready, q - 1)
                sp.dma_start(stage[:, q % 2], hankel(q)).then_inc(stage_in[q % 2], 16)

            for c in range(2, NCH):
                if c + 2 < NCH:
                    sp.wait_ge(x_transposed, c + 3 - XBUF)
                    sp.dma_start(xin[0:TIN, (c + 2) % XBUF], xr[c + 2]).then_inc(x_in[(c + 2) % XBUF], 16)
                if c == HLAG:
                    sp.wait_ge(kpad_out, 16)
                if c >= HLAG:
                    load_piece(c - HLAG)
            for q in range(NCH - HLAG, NHP):
                load_piece(q)
            assert E // 2 * FF >= (NHP - HRES) * HP * T
            sp.wait_ge(conv_mm, HRES * HP // CG)
            sp.dma_start(w1raw[:, E // 2:E], w1r[:, E // 2:E]).then_inc(w1_in[0], 16)
            sp.wait_ge(conv_mm, NCG)
            sp.dma_start(w1raw[:, 0:E // 2], w1r[:, 0:E // 2]).then_inc(w1_in[1], 16)
            tv = table[TROW:, :].rearrange("(b t) d -> t b d", t=TROW)[0:T]
            for g in range(NHB):
                sp.wait_ge(xn2_ready, g + 1)
                sp.wait_ge(xn2_act, g + 1)
                sp.wait_ge(xn2_pool, g + 1)
                for lo, hi in ((0, SPLIT), (SPLIT, T)):
                    sp.dma_start(tv[lo:hi, g * HB:(g + 1) * HB], XN[lo:hi, g * HB:(g + 1) * HB]).then_inc(table_out, 16)
            sp.wait_ge(table_out, 2 * NHB * 16)
            sp.wait_ge(x2_transposed, 2 * NHB)
            sp.dma_start(w2_sb, w2.rearrange("e d f -> d e f")).then_inc(w2_in, 16)
            sp.wait_ge(esum_clear, E // 2)
            sp.dma_start(table[0:TROW, :], esum[:, 0:D]).then_inc(zero_out, 16)
            pad = (TROW - T) * D
            sp.dma_start(bass.AP(table.tensor, (TROW + T) * D, [[TROW * D, B], [1, pad]]),
                         esum[0:B, 0:pad]).then_inc(zero_out, 16)
            ov = out.rearrange("b t d -> t b d")
            for g in range(NHB):
                sp.wait_ge(mixed, 2 * (g + 1))
                for lo, hi in ((0, SPLIT), (SPLIT, T)):
                    sp.dma_start(ov[lo:hi, g * HB:(g + 1) * HB], H[lo:hi, g * HB:(g + 1) * HB]).then_inc(out_done, 16)
            sp.wait_ge(out_done, 2 * NHB * 16)

        @block.gpsimd
        def _(pool):
            pool.memset(onef[:], 1.0)
            pool.memset(oneb[:], 1.0)
            pool.memset(minusb[:], -1.0)
            pool.memset(mhalf[:], -0.5)
            pool.memset(gateT[:], 0.0)
            pool.memset(kp[:], 0.0).then_inc(pool_const, 1)
            pool.wait_ge(pool_const, 1)
            pool.affine_select(out=ident[:], in_=onef[:], compare_op=ALU.is_equal, fill=0.0, base=0,
                               pattern=[[-1, 128]], channel_multiplier=1).then_inc(ident_ok, 1)
            pool.affine_select(out=trib[:], in_=onef[:], compare_op=ALU.is_gt, fill=0.0, base=0,
                               pattern=[[1, 128]], channel_multiplier=-1)
            pool.affine_select(out=bmask[:], in_=onef[:, 0:HB], compare_op=ALU.is_ge, fill=0.0, base=0,
                               pattern=[[-E, HB]], channel_multiplier=1).then_inc(pool_step, 1)
            pool.wait_ge(pool_step, 1)
            pool.affine_select(out=bmask[:], in_=bmask[:], compare_op=ALU.is_gt, fill=0.0, base=E,
                               pattern=[[E, HB]], channel_multiplier=-1)
            pool.iota(iotb[:], pattern=[[1, NT]], base=0, channel_multiplier=0,
                      allow_small_or_imprecise_dtypes=True).then_inc(pool_const, 1)

            def rstd(c, k):
                pool.wait_ge(ve1_ready, c + 1)
                nc.gpsimd.tensor_tensor(rs1[0:T, k], ve1[0:T, k], mhalf[0:T, 0:CB], ALU.pow).then_inc(rstd1, 1)

            with pool.Fori(0, NCH // 2) as i:
                for k in range(2):
                    rstd(i * 2 + k, k)
            for g in range(NHB):
                pool.wait_ge(ve2_ready, g + 1)
                if g >= 2:
                    pool.wait_ge(xn2_ready, g - 1)
                    pool.wait_ge(xn2_act, g - 1)
                nc.gpsimd.tensor_tensor(rs2[0:T, g % 2], ve2[0:T, g % 2], mhalf[0:T], ALU.pow).then_inc(rstd2, 1)
                pool.wait_ge(rstd2, g + 1)
                for q in range(HB - NORM_POOL, HB):
                    a = nc.gpsimd.tensor_scalar(XN[0:T, g * HB + q], H[0:T, g * HB + q], mm2[0:T, g % 2, 0, q:q + 1],
                                                rs2[0:T, g % 2, q:q + 1], ALU.subtract, ALU.mult)
                a.then_inc(xn2_pool, 1)
            for m in range(0, E, 2):
                if m == W1_FIRST:
                    pool.wait_ge(LW_ready, 1)
                    nc.gpsimd.tensor_tensor(L[0:T], LW[0:T], OH[1][0:T], ALU.mult).then_inc(picked_pool, 1)
                pool.wait_ge(w1_transposed, m + 2)
                e = (m + E // 2) % E
                pool.memset(esum[:, e * FF:(e + 2) * FF], 0.0).then_inc(esum_clear, 1)
            pool.wait_ge(hilo_ready, 1)
            for n in range(2 * B):
                if pool_made(n):
                    if n >= OBUF:
                        pool.wait_ge(code_mm, n - OBUF + 1)
                    nc.gpsimd.tensor_scalar(ohl[0:T, n % OBUF], iotb[0:T, 0:128], hilo[0:T, 1, n:n + 1], None,
                                            ALU.is_equal).then_inc(onehot_pool, 1)
            pool.wait_ge(idx_ready, 1)
            pool.wait_ge(table_out, 2 * NHB * 16)
            pool.wait_ge(zero_out, 32)
            for n in range(NT):
                if n >= GBUF:
                    pool.wait_ge(g_transposed, n - GBUF + 1)
                pool.indirect_dma_start(
                    out=G[:, n % GBUF, :], out_offset=None, in_=table[:, :],
                    in_offset=bass.IndirectOffsetOnAxis(ap=idx[:, n:n + 1], axis=0),
                ).then_inc(gathered[n % GBUF], 16)
            pool.wait_ge(esum_step, NT)
            for i, e in enumerate(in_parts):
                pool.wait_ge(sum_high, i + 1)
                if i >= 2:
                    pool.wait_ge(hsum_mm, in_parts[i - 2] + 1)
                nc.gpsimd.tensor_tensor(suml[:, i % 2], esum[:, e * FF:(e + 1) * FF], sumh[:, i % 2].bitcast(FP32),
                                        ALU.subtract).then_inc(sum_low, 1)

        @block.tensor
        def _(pe):
            def x_transposes(c, k, nth):
                pe.wait_ge(x_in[k], 16 * (nth + 1))
                if not (isinstance(c, int) and c == 0):
                    pe.wait_ge(xl_ready, c)
                for q in range(CB):
                    mm = nc.tensor.transpose(PX[:, q * TIN:(q + 1) * TIN], xin[0:TIN, k, q], ident[0:TIN, 0:TIN])
                mm.then_inc(x_transposed, 1)

            def gate_products(g, k, wpart, xpart, place):
                for w in range(WIN):
                    mm = nc.tensor.matmul(PG[g][:, 0:NV], wpart[:, w, g * D:(g + 1) * D], xpart[:, k, w:w + NV],
                                          start=(place == 0 and w == 0), stop=(place == 2 and w == WIN - 1))
                return mm

            def gates(c, k):
                pe.wait_ge(xl_ready, c + 1)
                for g in range(3):
                    if g == 2 and isinstance(c, int) and c == NCH - 1:
                        h_transposes(c - 1, (c - 1) % 2, False)
                    pe.wait_ge(gate_act, 3 * c - 3 + g + 1)
                    for place, (wpart, xpart) in enumerate(((wh, xh), (wh, xl), (wl, xh))):
                        mm = gate_products(g, k, wpart, xpart, place)
                    mm.then_inc(gate_mm, 1)

            def keep_warm(bank, n):
                for _ in range(n):
                    nc.tensor.matmul(bank[:, 0:128], onef[:], onef[:], start=True, stop=True)

            def h_transposes(c, k, first):
                pe.wait_ge(h_ready, c + 1)
                if not first:
                    pe.wait_ge(H_ready, c - 1)
                for q in range(CB):
                    mm = nc.tensor.transpose(PH[k][0:T, q * D:(q + 1) * D], hT[:, k, q * T:(q + 1) * T], ident[:])
                mm.then_inc(h_transposed, 1)

            def w1_transposes(m):
                e = (m + E // 2) % E
                pe.wait_ge(w1_in[m // (E // 2)], 16)
                if m >= 2:
                    pe.wait_ge(w1T_ready, m - 1)
                for q in range(4):
                    mm = nc.tensor.transpose(PT[m % 2][:, q * 128:(q + 1) * 128], w1raw[:, e, q], ident[:])
                mm.then_inc(w1_transposed, 1)

            def logits(n):
                pe.wait_ge(x2T_ready, n + 1)
                bank, at = P[n // 8], (n % 8) * 64
                for q in range(4):
                    lo = at + q * E
                    m = min(WARM, 512 - lo)
                    mm = nc.tensor.matmul(bank[0:T, lo:lo + m], x2T[:, n % 2, q], gateT[:, 0:m],
                                          start=True, stop=True)
                mm.then_inc(logits_mm, 1)

            pe.wait_ge(pool_const, 1)
            keep_warm(PW, 4)
            pe.wait_ge(ident_ok, 1)
            pe.wait_ge(pool_const, 2)
            x_transposes(0, 0, 0)
            keep_warm(PW, 3)
            for g in range(3):
                if g == 0:
                    pe.wait_ge(xh_ready, 1)
                    pe.wait_ge(wsplit, 1)
                gate_products(g, 0, wh, xh, 0)
                if g == 0:
                    pe.wait_ge(xl_ready, 1)
                gate_products(g, 0, wh, xl, 1)
                if g == 0:
                    pe.wait_ge(wsplit, 2)
                gate_products(g, 0, wl, xh, 2).then_inc(gate_mm, 1)
                if g == 0:
                    x_transposes(1, 1, 0)
            pe.wait_ge(ab_in, 96)
            for n in range(2):
                nc.tensor.transpose(PW[0:ORDER, n * 128:(n + 1) * 128], ab[:, n], ident[:])
            mm = nc.tensor.transpose(PW[:, 256:256 + E], gate_in[:], ident[0:E, 0:E])
            mm.then_inc(filt_mm, 1)
            x_transposes(2, 2, 0)
            gates(1, 1)
            pe.wait_ge(filt_ev, 1)
            for n, which in enumerate((1, 1, 0, 0)):
                mm = nc.tensor.matmul(PW[0:NF, n * 128:(n + 1) * 128], dft_sb[:, n * NF:(n + 1) * NF],
                                      abT[:, which], start=True, stop=True)
            mm.then_inc(filt_mm, 1)
            x_transposes(3, 3, 0)
            h_transposes(0, 0, True)
            for c in range(2, 4):
                if c > 2:
                    x_transposes(c + 1, (c + 1) % XBUF, (c + 1) // XBUF)
                gates(c, c % 2)
                h_transposes(c - 1, (c - 1) % 2, c == 2)
            pe.wait_ge(filt_step, FILT_LAST - 1)
            nc.tensor.matmul(PW[:, 0:T], fr[:, 10], idft_sb[:, 0:T], start=True, stop=False)
            nc.tensor.matmul(PW[:, 0:T], fr[:, 11], idft_sb[:, T:2 * T], start=False, stop=True).then_inc(filt_mm, 1)
            with pe.Fori(1, NCH // 4 - 1) as i:
                for k in range(4):
                    c = i * 4 + k
                    x_transposes(c + 1, (k + 1) % XBUF, i + (k + 1) // XBUF)
                    gates(c, k % 2)
                    h_transposes(c - 1, (k + 1) % 2, False)
            for c in range(NCH - 4, NCH):
                if c + 1 < NCH:
                    x_transposes(c + 1, (c + 1) % XBUF, (c + 1) // XBUF)
                gates(c, c % 2)
                if c + 1 < NCH:
                    h_transposes(c - 1, (c - 1) % 2, False)
            h_transposes(NCH - 1, (NCH - 1) % 2, False)
            keep_warm(PX, 12)
            pe.wait_ge(xn1_ready, NCH)
            for g in range(NCG):
                pe.wait_ge(hank_ready, g + 1)
                if g >= 3:
                    pe.wait_ge(gelu_done, g - 2)
                for j in range(CG):
                    c = g * CG + j
                    n = WARM if j < CG - 1 else B
                    mm = nc.tensor.matmul(PG[g % 3][0:T, j * B:j * B + n], hank[0:T, c // HP % HRES, c % HP],
                                          XF[0:T, c * B:c * B + n], start=True, stop=True)
                mm.then_inc(conv_mm, 1)

            for n in range(2 * NHB):
                pe.wait_ge(xn2_ready, n // 2 + 1)
                pe.wait_ge(xn2_act, n // 2 + 1)
                pe.wait_ge(xn2_pool, n // 2 + 1)
                if n >= 2:
                    pe.wait_ge(x2T_ready, n - 1)
                for q in range(4):
                    mm = nc.tensor.transpose(PR[n % 2][:, q * T:(q + 1) * T], XN[0:T, 4 * n + q], ident[0:T, 0:T])
                mm.then_inc(x2_transposed, 1)
                if n >= 1:
                    logits(n - 1)
            logits(2 * NHB - 1)
            pe.wait_ge(H_ready, NCH)
            for m in range(W1_FIRST):
                w1_transposes(m)
            pe.wait_ge(mask_ready, 4)
            by_expert = maskb[0:T].rearrange("p (b e) -> p e b", b=B)
            for h in range(2):
                nc.tensor.matmul(P[2 + h][:], oneb[0:T, :], by_expert[:, h * E // 2:(h + 1) * E // 2],
                                 start=True, stop=True).then_inc(prefix_mm, 1)
            for h in range(2):
                nc.tensor.matmul(P[h][0:T, :], trib[0:T, 0:T], maskb[0:T, h * 512:(h + 1) * 512], start=True, stop=False)
                mm = nc.tensor.matmul(P[h][0:T, :], minusb[0:T, 0:T], maskb[0:T, h * 512:(h + 1) * 512],
                                      start=False, stop=True)
            mm.then_inc(prefix_mm, 1)
            for m in range(W1_FIRST, E):
                w1_transposes(m)
            pe.wait_ge(ends_ready, 1)
            nc.tensor.matmul(P[5][0:1, 0:NT], onef[0:E - 1, 0:1], ends[:], start=True, stop=True).then_inc(eid_mm, 1)

            pe.wait_ge(w1T_ready, E)
            keep_warm(P[4], 15)
            pe.wait_ge(hilo_ready, 1)
            nc.tensor.transpose(P[0][:, 0:T], hilo[0:T, 1], ident[0:T, 0:T]).then_inc(lo_mm, 1)
            pe.wait_ge(loT_ready, 1)

            def distances(a):
                if a >= 3:
                    pe.wait_ge(act_square, a - 2)
                n, bank = on_act[a] * OG, PD[a % 3]
                nc.tensor.matmul(bank[0:T, :], oneb[:, 0:T], iota1b.unsqueeze(1).to_broadcast([128, OG, 128]),
                                 start=True, stop=False)
                nc.tensor.matmul(bank[0:T, :], loT[:], minus1b[:, n:n + OG].unsqueeze(2).to_broadcast([128, OG, 128]),
                                 start=False, stop=True).then_inc(distance_mm, 1)

            for a in range(2):
                distances(a)
            for n in range(2 * B):
                j = n // OG
                if n % OG == 0 and not pool_made(n) and on_act.index(j) + 2 < len(on_act):
                    distances(on_act.index(j) + 2)
                pe.wait_ge(onehot, n + 1)
                if pool_made(n):
                    pe.wait_ge(onehot_pool, sum(pool_made(m) for m in range(n)) + 1)
                elif n % OG == 0:
                    pe.wait_ge(onehot_act, on_act.index(j) + 1)
                nc.tensor.matmul(P[4][:, 0:NT], ohl[0:T, n % OBUF], ohh[0:T, n % OBUF, 0:NT],
                                 start=(n == 0), stop=(n == 2 * B - 1)).then_inc(code_mm, 1)

            def g_transpose(n, k, nth):
                pe.wait_ge(gathered[k], 16 * (nth + 1))
                if not (isinstance(n, int) and n < 2):
                    pe.wait_ge(GT_ready, n - 1)
                nc.tensor.transpose(P[4 + k % 2][:, 0:SLOT], G[:, k], ident[:]).then_inc(g_transposed, 1)

            regs = [pe.alloc_register(f"pe_expert{k}") for k in range(UNROLL)]

            def experts_of(n):
                pe.load(regs, eid[0:1, bass.ds(n, UNROLL)])

            def expert(n, k, reg, first):
                e = pe.snap(regs[reg], min_val=0, max_val=E - 1)
                pe.wait_ge(GT_ready, n + 1)
                if not first:
                    pe.wait_ge(silu_done, n - 3)
                nc.tensor.matmul(P[k % 4][:, :], GT[:, k % 2], w1T[:, bass.ds(e * FF, FF)],
                                 start=True, stop=True).then_inc(expert_mm, 1)

            pe.wait_ge(eid_ready, 1)
            experts_of(0)
            keep_warm(P[0], 11)
            g_transpose(0, 0, 0)
            for n in range(1, UNROLL + 1):
                g_transpose(n, n % GBUF, n // GBUF)
                if n in RT_AT:
                    pe.wait_ge(R_ready, 1)
                    h = RT_AT.index(n)
                    for g in range(4):
                        b = (4 * h + g) * HB
                        mm = nc.tensor.transpose(P[6 + h][:, g * T:(g + 1) * T],
                                                 L[0:T, b:b + HB].rearrange("p b e -> p (b e)"), ident[0:T, 0:T])
                    mm.then_inc(RT_mm, 1)
                expert(n - 1, n - 1, n - 1, n - 1 < 4)
            with pe.Fori(1, NT // UNROLL) as i:
                experts_of(i * UNROLL)
                for k in range(UNROLL - 1):
                    g_transpose(i * UNROLL + (k + 1), (k + 1) % GBUF, i * (UNROLL // GBUF) + (k + 1) // GBUF)
                    expert(i * UNROLL + k, k, k, False)
                g_transpose(i * UNROLL + UNROLL, 0, i * (UNROLL // GBUF) + UNROLL // GBUF)
                expert(i * UNROLL + (UNROLL - 1), UNROLL - 1, UNROLL - 1, False)
            rest = NT // UNROLL * UNROLL
            pe.load(regs[0:NT - rest], eid[0:1, rest:NT])
            for n in range(rest, NT):
                if n + 1 < NT:
                    g_transpose(n + 1, (n + 1) % GBUF, (n + 1) // GBUF)
                expert(n, n % UNROLL, n - rest, False)

            pe.wait_ge(esum_step, NT)
            for e in range(E):
                if e >= 4:
                    pe.wait_ge(y_step, e - 3)
                if e not in in_parts:
                    nc.tensor.matmul(P[e % 4][:, :], onef[:], esum[:, e * FF:(e + 1) * FF],
                                     start=True, stop=True).then_inc(hsum_mm, 1)
                else:
                    k = in_parts.index(e) % 2
                    pe.wait_ge(sum_low, in_parts.index(e) + 1)
                    nc.tensor.matmul(P[e % 4][:, :], oner[:], sumh[:, k], start=True, stop=False)
                    nc.tensor.matmul(P[e % 4][:, :], oner[:], suml[:, k], start=False, stop=True).then_inc(hsum_mm, 1)
            pe.wait_ge(y_step, E + 1)
            for n in range(2):
                mm = nc.tensor.transpose(P[4 + n][:, 0:128], yrep.rearrange("p b e -> p (b e)"), ident[:])
            mm.then_inc(y_transposed, 1)
            keep_warm(P[6], 5)
            pe.wait_ge(RT_low, 2)
            for n in range(2 * NHB):
                if n >= 4:
                    pe.wait_ge(mixed, n - 3)
                half = slice(n % 2 * 4, n % 2 * 4 + 4)
                if n < 2:
                    pe.wait_ge(yh_ready, 4 * (n + 1))
                for place, (rpart, ypart) in enumerate(((RTh, yh), (RTl, yh), (RTh, yl))):
                    if n < 2 and place == 2:
                        pe.wait_ge(yl_ready, n + 1)
                    mm = nc.tensor.matmul(P[n % 4][0:T, :], rpart[:, n // 8, n // 2 % 4],
                                          ypart[:, half].rearrange("p b d -> p (b d)"),
                                          start=(place == 0), stop=(place == 2))
                mm.then_inc(mix_mm, 1)

        @block.scalar
        def _(act):
            def gate_acts(c, k, first):
                for g, (dst, func) in enumerate(((zg, ACT.Tanh), (fg, ACT.Sigmoid), (og, ACT.Sigmoid))):
                    if g == 2 and isinstance(c, int) and c == NCH - 1:
                        copy_H(c - 1, (c - 1) % 2)
                    act.wait_ge(gate_mm, 3 * c + g + 1)
                    if not first and g == 0:
                        act.wait_ge(h_ready, c - 1)
                    src = PG[g][:, 0:XW].rearrange("p (b t) -> p b t", b=CB)[:, :, 0:T]
                    nc.scalar.activation(dst[:, k].rearrange("p (b t) -> p b t", b=CB), src, func).then_inc(gate_act, 1)

            def copy_xT(c, k, first):
                act.wait_ge(x_transposed, c + 1)
                if not first:
                    act.wait_ge(gate_mm, 3 * c - 3)
                nc.scalar.copy(xh[:, k], PX[:, 0:XW]).then_inc(xh_ready, 1)

            def copy_H(c, k):
                act.wait_ge(h_transposed, c + 1)
                nc.scalar.copy(H[0:T, bass.ds(c * CB, CB)].rearrange("p b c -> p (b c)") if not isinstance(c, int)
                               else H[0:T, c * CB:(c + 1) * CB].rearrange("p b c -> p (b c)"),
                               PH[k][0:T, :]).then_inc(H_ready, 1)

            def copy_w1T(m):
                e = (m + E // 2) % E
                act.wait_ge(w1_transposed, m + 1)
                nc.scalar.copy(w1T[:, e * FF:(e + 1) * FF], PT[m % 2][:, :]).then_inc(w1T_ready, 1)

            def filters(q, k, nth):
                act.wait_ge(stage_in[k], 16 * (nth + 1))
                if isinstance(q, int):
                    dst = hank[:, q % HRES]
                else:
                    dst = BIG[:, bass.ds(q * (HP * T), HP * T)].rearrange("p (c t) -> p c t", c=HP)
                nc.scalar.copy(dst, stage[:, k, :, ::-1]).then_inc(hank_ready, 1)

            copy_xT(0, 0, True)
            copy_xT(1, 1, True)
            gate_acts(0, 0, True)
            act.wait_ge(filt_mm, 1)
            act.wait_ge(pool_const, 1)
            nc.scalar.copy(gateT[:, 0:E], PW[:, 256:256 + E])
            nc.scalar.copy(abT[:].rearrange("p a c -> p (a c)"), PW[0:ORDER, 0:256]).then_inc(filt_ev, 1)
            copy_xT(2, 0, False)
            gate_acts(1, 1, True)
            copy_xT(3, 1, False)
            copy_H(0, 0)
            for c in range(2, 4):
                if c > 2:
                    copy_xT(c + 1, (c + 1) % 2, False)
                gate_acts(c, c % 2, False)
                copy_H(c - 1, (c - 1) % 2)
            act.wait_ge(filt_step, FILT_LAST)
            act.dma_start(kpad, kp[:]).then_inc(kpad_out, 16)
            with act.Fori(1, NCH // 4 - 1) as i:
                for k in range(4):
                    c = i * 4 + k
                    copy_xT(c + 1, (k + 1) % 2, False)
                    gate_acts(c, k % 2, False)
                    copy_H(c - 1, (k + 1) % 2)
                    filters(c - HLAG, k % 2, i * 2 + k // 2 - HLAG // 2)
            for c in range(NCH - 4, NCH):
                if c + 1 < NCH:
                    copy_xT(c + 1, (c + 1) % 2, False)
                gate_acts(c, c % 2, False)
                if c + 1 < NCH:
                    copy_H(c - 1, (c - 1) % 2)
                filters(c - HLAG, c % 2, (c - HLAG) // 2)
            copy_H(NCH - 1, (NCH - 1) % 2)

            assert NCH - HLAG == HRES and HP == CG
            act.wait_ge(h_ready, NCH)
            nc.scalar.activation(zg[0:T, 0, 0:D], fg[0:T, 0, 0:D], ACT.Gelu_apprx_tanh)
            for g in range(NCG):
                act.wait_ge(conv_mm, g + 1)
                if g >= 2:
                    act.wait_ge(H_added, g - 1)
                nc.scalar.activation(gl[0:T, g % 2].rearrange("p c b -> p (c b)"), PG[g % 3][0:T, :],
                                     ACT.Gelu_apprx_tanh).then_inc(gelu_done, 1)

            def norm2(g):
                act.wait_ge(nmr_ready, g + 1)
                for q in range(dve_norms(g), HB - NORM_POOL):
                    a = nc.scalar.activation(XN[0:T, g * HB + q], H[0:T, g * HB + q], ACT.Identity,
                                             bias=nmr[0:T, g % 2, q:q + 1], scale=rs2[0:T, g % 2, q:q + 1])
                a.then_inc(xn2_act, 1)

            def copy_L(h):
                act.wait_ge(logits_mm, (h + 1) * NHB)
                nc.scalar.copy(L[0:T, h * 32:(h + 1) * 32].rearrange("p b e -> p (b e)"), P[h][0:T, :]).then_inc(L_ready, 1)

            norm2(0)
            for n in range(2 * NHB):
                if n % 2 == 0 and n // 2 + 1 < NHB:
                    norm2(n // 2 + 1)
                if n == NHB + 2:
                    copy_L(0)
                act.wait_ge(x2_transposed, n + 1)
                if n >= 2:
                    act.wait_ge(logits_mm, n - 1)
                nc.scalar.copy(x2T[:, n % 2].rearrange("p b t -> p (b t)"), PR[n % 2][:, 0:4 * T]).then_inc(x2T_ready, 1)
            copy_L(1)

            for m in range(E):
                copy_w1T(m)
            act.wait_ge(diff_ready, 1)
            nc.scalar.activation(wgt[0:T, 1], wgt[0:T, 0], ACT.Sigmoid)
            nc.scalar.activation(wgt[0:T, 2], wgt[0:T, 0], ACT.Sigmoid, scale=-1.0).then_inc(wgt_ready, 1)
            nc.scalar.mul(minus1b[:], ident[:], -1.0)
            act.wait_ge(pool_const, 2)
            act.wait_ge(const_in, 32)
            nc.scalar.mul(iota1b[:], iotb[:, 0:128], 1.0 / 128)
            act.wait_ge(lo_mm, 1)
            nc.scalar.copy(loT[:], P[0][:, 0:T]).then_inc(loT_ready, 1)

            def square(a):
                act.wait_ge(distance_mm, a + 1)
                if a >= 3:
                    act.wait_ge(onehot_act, a - 2)
                nc.scalar.activation(ohq[0:T, a % 3], PD[a % 3][0:T, :], ACT.Square).then_inc(act_square, 1)

            square(0)
            for a, j in enumerate(on_act):
                if a + 1 < len(on_act):
                    square(a + 1)
                at = j * OG % OBUF
                if j * OG >= OBUF:
                    act.wait_ge(code_mm, j * OG + OG - OBUF)
                act.wait_ge(act_square, a + 1)
                nc.scalar.activation(ohl[0:T, at:at + OG].rearrange("p k s -> p (k s)"), ohq[0:T, a % 3], ACT.Relu,
                                     bias=code_sb[0:T, EXPO:EXPO + 1], scale=-2.0).then_inc(onehot_act, 1)
            act.wait_ge(onehot_act, len(on_act))
            nc.scalar.activation(ohq[0:T, 0], ohq[0:T, 1], ACT.Silu)

            def copy_GT(n, k, first):
                act.wait_ge(g_transposed, n + 1)
                if not first:
                    act.wait_ge(expert_mm, n - 1)
                nc.scalar.copy(GT[:, k % 2], P[4 + k % 2][:, 0:SLOT]).then_inc(GT_ready, 1)

            def silu(n, k, first):
                act.wait_ge(expert_mm, n + 1)
                if not first:
                    act.wait_ge(esum_step, n - 3)
                nc.scalar.activation(S[:, k % 4], P[k % 4][:, :], ACT.Silu).then_inc(silu_done, 1)

            for n in range(UNROLL + 1):
                copy_GT(n, n, n < 2)
                if n == 2:
                    act.wait_ge(R_ready, 1)
                if n >= 2:
                    silu(n - 2, n - 2, n - 2 < 4)
                if n in RT_AT:
                    h = RT_AT.index(n)
                    act.wait_ge(RT_mm, h + 1)
                    nc.scalar.copy(xh[:, h, 0:4 * T], P[6 + h][:, 0:4 * T]).then_inc(RT_high, 1)
            silu(UNROLL - 1, UNROLL - 1, False)
            with act.Fori(1, NT // UNROLL) as i:
                for k in range(UNROLL):
                    copy_GT(i * UNROLL + (k + 1), k + 1, False)
                    silu(i * UNROLL + k, k, False)
            for n in range(NT // UNROLL * UNROLL, NT):
                if n + 1 < NT:
                    copy_GT(n + 1, n + 1, False)
                silu(n, n % UNROLL, False)

            nc.scalar.copy(oner[:], onef[:])
            act.wait_ge(esum_step, NT)
            for i, e in enumerate(in_parts):
                if i >= 2:
                    act.wait_ge(hsum_mm, in_parts[i - 2] + 1)
                nc.scalar.copy(sumh[:, i % 2], esum[:, e * FF:(e + 1) * FF]).then_inc(sum_high, 1)

            act.wait_ge(y_transposed, 1)
            for b in range(HB):
                nc.scalar.mul(yh[:, b], P[4][:, 0:128], bmask[:, b:b + 1]).then_inc(yh_ready, 1)

        @block.vector
        def _(dve):
            v = nc.vector

            def moments(st, m, ve, done, count, ready):
                v.tensor_tensor(m[:, 1], st[:, :, 1], st[:, :, 4], ALU.subtract)
                v.tensor_tensor(m[:, 2], st[:, :, 2], st[:, :, 5], ALU.add)
                v.tensor_tensor(m[:, 0], st[:, :, 1], st[:, :, 4], ALU.add).then_inc(done, 1)
                dve.wait_ge(done, count + 1)
                v.scalar_tensor_tensor(out=m[:, 1], in0=m[:, 1], scalar=0.25, in1=m[:, 1],
                                       op0=ALU.mult, op1=ALU.mult)
                v.tensor_scalar(m[:, 2], m[:, 2], 1.0 / D, EPS, ALU.mult, ALU.add).then_inc(done, 1)
                dve.wait_ge(done, count + 2)
                v.tensor_scalar(m[:, 0], m[:, 0], 0.5, None, ALU.mult).then_inc(done, 1)
                v.tensor_tensor(ve, m[:, 1], m[:, 2], ALU.add).then_inc(ready, 1)

            def cell(c, k):
                dve.wait_ge(gate_act, 3 * c + 3)
                v.scalar_tensor_tensor(out=cc[:, k], in0=fg[:, k], scalar=-1.0, in1=zg[:, k],
                                       op0=ALU.add, op1=ALU.mult).then_inc(cell_step, 1)
                dve.wait_ge(cell_step, 3 * c + 1)
                v.memset(fg[:, k].rearrange("p (b t) -> p b t", b=CB)[:, :, 0:1], 0.0).then_inc(cell_step, 1)
                dve.wait_ge(cell_step, 3 * c + 2)
                v.tensor_tensor_scan(cc[:, k], fg[:, k], cc[:, k], 0.0, ALU.mult, ALU.subtract).then_inc(cell_step, 1)
                dve.wait_ge(cell_step, 3 * c + 3)
                if not (isinstance(c, int) and c < 2):
                    dve.wait_ge(h_transposed, c - 1)
                v.tensor_tensor(hT[:, k], cc[:, k], og[:, k], ALU.mult).then_inc(h_ready, 1)

            def H_of(c, q):
                at = c * CB + q
                return H[0:T, at] if isinstance(at, int) else H[0:T, bass.ds(at, 1)].rearrange("p a c -> p (a c)")

            def stats(c, k):
                dve.wait_ge(H_ready, c + 1)
                for q in range(CB):
                    a = v.bn_stats(st1[0:T, k, q], H_of(c, q))
                a.then_inc(bn1, 1)
                dve.wait_ge(bn1, 4 * c + 1)
                moments(st1[0:T, k], mm1[0:T, k], ve1[0:T, k], bn1, 4 * c + 1, ve1_ready)

            def norm(c, k):
                dve.wait_ge(rstd1, c + 1)
                for q in range(CB):
                    at = c * CB + q
                    dst = XC[0:T, :, at] if isinstance(at, int) else XC[0:T, :, bass.ds(at, 1)].rearrange("p c a -> p (c a)")
                    a = v.tensor_scalar(dst, H_of(c, q), mm1[0:T, k, 0, q:q + 1], rs1[0:T, k, q:q + 1],
                                        ALU.subtract, ALU.mult)
                a.then_inc(xn1_ready, 1)

            def low_part(c, k):
                dve.wait_ge(xh_ready, c + 1)
                v.tensor_tensor(xl[:, k], PX[:, 0:XW], xh[:, k].bitcast(FP32), ALU.subtract).then_inc(xl_ready, 1)

            dve.wait_ge(wk_in, 16)
            v.tensor_copy(wh[:], wk[:]).then_inc(wsplit, 1)
            dve.wait_ge(wsplit, 1)
            low_part(0, 0)
            v.tensor_tensor(wl[:], wk[:], wh[:].bitcast(FP32), ALU.subtract).then_inc(wsplit, 1)
            low_part(1, 1)
            cell(0, 0)
            low_part(2, 0)
            cell(1, 1)
            low_part(3, 1)
            stats(0, 0)
            steps = [0]

            def fstep(ins):
                steps[0] += 1
                ins.then_inc(filt_step, 1)
                dve.wait_ge(filt_step, steps[0])

            dve.wait_ge(filt_mm, 2)
            fstep(v.tensor_copy(fr[:, 0:4].rearrange("p a c -> p (a c)"), PW[0:NF, :]))
            fstep(v.tensor_scalar(fr[:, 2], fr[:, 2], 1.0, None, ALU.add))
            fstep(v.tensor_tensor(fr[:, 4:6], fr[:, 2:4], fr[:, 2:4], ALU.mult))
            fstep(v.tensor_tensor(fr[:, 6], fr[:, 4], fr[:, 5], ALU.add))
            fstep(v.reciprocal(fr[:, 7], fr[:, 6]))
            v.tensor_tensor(fr[:, 4], fr[:, 0], fr[:, 2], ALU.mult)
            v.tensor_tensor(fr[:, 5], fr[:, 1], fr[:, 3], ALU.mult)
            v.tensor_tensor(fr[:, 8], fr[:, 1], fr[:, 2], ALU.mult)
            fstep(v.tensor_tensor(fr[:, 9], fr[:, 0], fr[:, 3], ALU.mult))
            fstep(v.tensor_tensor(fr[:, 4], fr[:, 4], fr[:, 5], ALU.add))
            fstep(v.tensor_tensor(fr[:, 8], fr[:, 8], fr[:, 9], ALU.subtract))
            low_part(4, 0)
            cell(2, 0)
            stats(1, 1)
            fstep(v.tensor_tensor(fr[:, 10], fr[:, 4], fr[:, 7], ALU.mult))
            fstep(v.tensor_tensor(fr[:, 11], fr[:, 8], fr[:, 7], ALU.mult))
            steps[0] += 1
            v.tensor_copy(fr[:, 6], fr[:, 7]).then_inc(filt_step, 1)
            dve.wait_ge(filt_step, steps[0])
            norm(0, 0)
            cell(3, 1)
            dve.wait_ge(filt_mm, 3)
            dve.wait_ge(pool_const, 1)
            dve.wait_ge(ab_in, 96)
            v.tensor_copy(kp[:, 0:T - 1], PW[:, 0:T - 1])
            v.tensor_scalar(kp[:, T - 1:T], PW[:, T - 1:T], h0c[:, 0:1], None, ALU.add).then_inc(filt_step, 1)
            assert steps[0] + 1 == FILT_LAST, steps[0]
            stats(2, 0)
            norm(1, 1)
            with dve.Fori(1, NCH // 4 - 1) as i:
                for k in range(4):
                    c = i * 4 + k
                    low_part(c + 1, (k + 1) % 2)
                    cell(c, k % 2)
                    stats(c - 1, (k + 1) % 2)
                    norm(c - 2, k % 2)
            for c in range(NCH - 4, NCH - 1):
                low_part(c + 1, (c + 1) % 2)
                cell(c, c % 2)
                stats(c - 1, (c - 1) % 2)
                norm(c - 2, c % 2)
            stats(NCH - 2, NCH % 2)
            cell(NCH - 1, (NCH - 1) % 2)
            norm(NCH - 3, (NCH - 1) % 2)
            stats(NCH - 1, (NCH - 1) % 2)
            norm(NCH - 2, NCH % 2)
            norm(NCH - 1, (NCH - 1) % 2)

            dve.wait_ge(H_ready, NCH)
            for g in range(NCG):
                q = HRES + g
                if q < NHP:
                    dve.wait_ge(stage_in[q % 2], 16 * (q // 2 + 1))
                    dve.wait_ge(conv_mm, g + 1)
                    v.tensor_copy(hank[:, g], stage[:, q % 2, :, ::-1]).then_inc(hank_ready, 1)
                dve.wait_ge(gelu_done, g + 1)
                hv = H[0:T, :, g * CG:(g + 1) * CG].rearrange("p b c -> p c b")
                v.tensor_tensor(hv, hv, gl[0:T, g % 2], ALU.add).then_inc(H_added, 1)
            dve.wait_ge(H_added, NCG)

            def norm2_start(g):
                dve.wait_ge(rstd2, g + 1)
                if g >= 2:
                    dve.wait_ge(xn2_act, g - 1)
                v.scalar_tensor_tensor(out=nmr[0:T, g % 2], in0=mm2[0:T, g % 2, 0], scalar=-1.0, in1=rs2[0:T, g % 2],
                                       op0=ALU.mult, op1=ALU.mult).then_inc(nmr_ready, 1)

            def norm2(g, q):
                return v.tensor_scalar(XN[0:T, g * HB + q], H[0:T, g * HB + q], mm2[0:T, g % 2, 0, q:q + 1],
                                       rs2[0:T, g % 2, q:q + 1], ALU.subtract, ALU.mult)

            for g in range(NHB):
                for q in range(HB):
                    a = v.bn_stats(st2[0:T, g % 2, q], H[0:T, g * HB + q])
                a.then_inc(bn2, 1)
                if g >= 1:
                    norm2_start(g - 1)
                if g >= 2:
                    dve.wait_ge(xn2_pool, g - 1)
                dve.wait_ge(bn2, 3 * g + 1)
                st, m = st2[0:T, g % 2], mm2[0:T, g % 2]
                v.tensor_tensor(m[:, 1], st[:, :, 1], st[:, :, 4], ALU.subtract)
                v.tensor_tensor(m[:, 2], st[:, :, 2], st[:, :, 5], ALU.add)
                v.tensor_tensor(m[:, 0], st[:, :, 1], st[:, :, 4], ALU.add).then_inc(bn2, 1)
                if g >= 1:
                    norm2(g - 1, 0)
                dve.wait_ge(bn2, 3 * g + 2)
                v.scalar_tensor_tensor(out=m[:, 1], in0=m[:, 1], scalar=0.25, in1=m[:, 1], op0=ALU.mult, op1=ALU.mult)
                v.tensor_scalar(m[:, 0], m[:, 0], 0.5, None, ALU.mult)
                v.tensor_scalar(m[:, 2], m[:, 2], 1.0 / D, EPS, ALU.mult, ALU.add).then_inc(bn2, 1)
                if g >= 1:
                    norm2(g - 1, 1).then_inc(xn2_ready, 1)
                dve.wait_ge(bn2, 3 * g + 3)
                v.tensor_tensor(ve2[0:T, g % 2], m[:, 1], m[:, 2], ALU.add).then_inc(ve2_ready, 1)
            norm2_start(NHB - 1)
            for q in range(NORM_DVE_LAST):
                a = norm2(NHB - 1, q)
            a.then_inc(xn2_ready, 1)
            assert NORM_DVE == 2

            rs = [0]

            def step(ins):
                rs[0] += 1
                ins.then_inc(route_step, 1)
                dve.wait_ge(route_step, rs[0])

            dve.wait_ge(pool_const, 2)
            dve.wait_ge(const_in, 32)

            step(v.tensor_copy(rankb[:], rank_sb[:]))
            QB = B // 4
            rk = rankb[0:T].unsqueeze(1).to_broadcast([T, QB, E])
            mb = maskb[0:T].rearrange("p (b e) -> p b e", b=B)
            for h in range(2):
                dve.wait_ge(L_ready, h + 1)
                last = [0, 0]

                def by_turns(op, done=route_step):
                    for q in range(2):
                        if last[q]:
                            dve.wait_ge(route_step, last[q])
                        ins = op(slice((2 * h + q) * QB, (2 * h + q + 1) * QB)).then_inc(done, 1)
                        if done is route_step:
                            rs[0] += 1
                            last[q] = rs[0]

                def each(part, qb):
                    return part[:, qb].unsqueeze(2).to_broadcast([T, QB, E])

                for k, src in enumerate((L, LW)):
                    by_turns(lambda qb: v.tensor_reduce(mx[0:T, k, qb], src[0:T, qb], AX.X, ALU.max))
                    by_turns(lambda qb: v.tensor_tensor(OH[k][0:T, qb], src[0:T, qb], each(mx[0:T, k], qb), ALU.is_equal))
                    by_turns(lambda qb: v.tensor_tensor(OH[k][0:T, qb], OH[k][0:T, qb], rk, ALU.mult))
                    by_turns(lambda qb: v.tensor_reduce(firstb[0:T, k, qb], OH[k][0:T, qb], AX.X, ALU.max))
                    by_turns(lambda qb: v.tensor_tensor(OH[k][0:T, qb], rk, each(firstb[0:T, k], qb), ALU.is_equal))
                    if k == 0:
                        by_turns(lambda qb: v.scalar_tensor_tensor(out=LW[0:T, qb], in0=OH[0][0:T, qb], scalar=NEG,
                                                                   in1=L[0:T, qb], op0=ALU.mult, op1=ALU.add))
                by_turns(lambda qb: v.tensor_tensor(mb[:, qb], OH[0][0:T, qb], OH[1][0:T, qb], ALU.add), mask_ready)
            v.tensor_tensor(wgt[0:T, 0], mx[0:T, 0], mx[0:T, 1], ALU.subtract).then_inc(diff_ready, 1)
            dve.wait_ge(prefix_mm, 1)
            flat = cum.rearrange("p e b -> p (e b)")
            zeros = gateT[:, E:E + 1].to_broadcast([128, 512])
            step(v.tensor_tensor_scan(flat[:, 0:512], P[2][:], zeros, 0.0, ALU.add, ALU.max))
            dve.wait_ge(prefix_mm, 2)
            step(v.tensor_tensor_scan(flat[:, 512:1024], P[3][:], zeros, flat[:, 511:512], ALU.add, ALU.max))
            step(v.tensor_copy(small[:, 0], cum[:, :, B - 1]))
            v.tensor_copy(small[:, 1, 0:1], small[:, 0, 0:1])
            step(v.tensor_tensor(small[:, 1, 1:E], small[:, 0, 1:E], small[:, 0, 0:E - 1], ALU.subtract))
            step(v.tensor_scalar(smi[:, 0], small[:, 1], float(SLOT - 1), None, ALU.add))
            step(v.tensor_scalar(smi[:, 1], smi[:, 0], 7, None, ALU.arith_shift_right))
            step(v.tensor_copy(small[:, 4], smi[:, 1]))
            step(v.tensor_tensor_scan(small[:, 2], small[:, 4], small[:, 4], 0.0, ALU.add, ALU.max))
            v.tensor_scalar(small[:, 3, 0:1], small[:, 0, 0:1], 0.0, None, ALU.mult)
            step(v.scalar_tensor_tensor(out=small[:, 3, 1:E], in0=small[:, 2, 0:E - 1], scalar=float(SLOT),
                                        in1=small[:, 0, 0:E - 1], op0=ALU.mult, op1=ALU.subtract))
            step(v.tensor_tensor(cum[:], cum[:], small[:, 3].unsqueeze(2).to_broadcast([128, E, B]), ALU.add))
            step(v.tensor_tensor(y[0:E], small[0:E, 2], ident[0:E, 0:E], ALU.mult))
            step(v.tensor_reduce(small[0:E, 4, 0:1], y[0:E], AX.X, ALU.add))
            v.tensor_scalar(ends[:], iotb[0:E - 1, :], small[0:E - 1, 4, 0:1], None, ALU.is_ge).then_inc(ends_ready, 1)
            dve.wait_ge(prefix_mm, 3)
            for h in range(2):
                a = v.tensor_tensor(LW[0:T, h * 32:(h + 1) * 32],
                                    P[h][0:T, :].rearrange("p (b e) -> p b e", b=32),
                                    cum[0:T, :, h * 32:(h + 1) * 32].rearrange("p e b -> p b e"), ALU.add)
            a.then_inc(LW_ready, 1)
            dve.wait_ge(LW_ready, 1)
            step(v.tensor_tensor(picked[0:T], LW[0:T], OH[0][0:T], ALU.mult))
            v.tensor_reduce(pos[0:T, 0:B], picked[0:T], AX.X, ALU.add)
            dve.wait_ge(picked_pool, 1)
            step(v.tensor_reduce(pos[0:T, B:2 * B], L[0:T], AX.X, ALU.add))
            step(v.tensor_copy(posi[0:T, 0], pos[0:T]))
            v.tensor_scalar(posi[0:T, 1], posi[0:T, 0], 7, None, ALU.arith_shift_right)
            step(v.tensor_scalar(posi[0:T, 2], posi[0:T, 0], SLOT - 1, None, ALU.bitwise_and))
            v.tensor_copy(hilo[0:T], posi[0:T, 1:3]).then_inc(hilo_ready, 1)
            dve.wait_ge(hilo_ready, 1)

            dve.wait_ge(eid_mm, 1)
            v.tensor_copy(eid[:], P[5][0:1, 0:NT]).then_inc(eid_ready, 1)

            for n in range(2 * B):
                if n >= OBUF:
                    dve.wait_ge(code_mm, n - OBUF + 1)
                iota_hi, tile = iotb[0:T], hilo[0:T, 0, n:n + 1]
                if pool_made(n):
                    v.tensor_scalar(ohh[0:T, n % OBUF, 0:NT], iota_hi, tile, code_sb[0:T, n % B:n % B + 1],
                                    ALU.is_equal, ALU.mult).then_inc(onehot, 1)
                else:
                    v.tensor_scalar(ohh[0:T, n % OBUF, 0:NT], iota_hi, tile, 2.0 ** (n % B - EXPO),
                                    ALU.is_equal, ALU.mult).then_inc(onehot, 1)
            dve.wait_ge(code_mm, 2 * B)
            step(v.tensor_scalar(idx[:], P[4][:, 0:NT].bitcast(I32), 16, None, ALU.arith_shift_right))
            v.tensor_scalar(idx[:], idx[:], float((127 - EXPO - 1) * TROW), 0.0, ALU.subtract, ALU.max).then_inc(idx_ready, 1)
            dve.wait_ge(wgt_ready, 1)
            for k, dst in enumerate((L[0:T], picked[0:T])):
                step(v.tensor_tensor(dst, OH[k][0:T], wgt[0:T, 1 + k].unsqueeze(2).to_broadcast([T, B, E]), ALU.mult))
            v.tensor_tensor(L[0:T], L[0:T], picked[0:T], ALU.add).then_inc(R_ready, 1)
            step(v.tensor_scalar(small[:, 5], small[:, 1], 1.0, None, ALU.max))
            step(v.reciprocal(small[:, 6], small[:, 5]))

            dve.wait_ge(esum_clear, E // 2)
            dve.wait_ge(eid_ready, 1)

            regs = [dve.alloc_register(f"dve_expert{k}") for k in range(UNROLL)]

            def accumulate(n, k, reg, first):
                e = dve.snap(regs[reg], min_val=0, max_val=E - 1)
                dve.wait_ge(silu_done, n + 1)
                if not first:
                    dve.wait_ge(esum_step, n)
                at = esum[:, bass.ds(e * FF, FF)]
                v.tensor_tensor(at, at, S[:, k % 4], ALU.add).then_inc(esum_step, 1)

            dve.load(regs, eid[0:1, 0:UNROLL])
            for n in range(UNROLL):
                accumulate(n, n, n, n == 0)
                if n in RT_AT:
                    h = RT_AT.index(n)
                    dve.wait_ge(RT_high, h + 1)
                    v.tensor_tensor(xl[:, h, 0:4 * T], P[6 + h][:, 0:4 * T], xh[:, h, 0:4 * T].bitcast(FP32),
                                    ALU.subtract).then_inc(RT_low, 1)
            with dve.Fori(1, NT // UNROLL) as i:
                dve.load(regs, eid[0:1, bass.ds(i * UNROLL, UNROLL)])
                for k in range(UNROLL):
                    accumulate(i * UNROLL + k, k, k, False)
            rest = NT // UNROLL * UNROLL
            dve.load(regs[0:NT - rest], eid[0:1, rest:NT])
            for n in range(rest, NT):
                accumulate(n, n, n - rest, False)

            dve.wait_ge(w2_in, 16)
            for e in range(E):
                dve.wait_ge(hsum_mm, e + 1)
                if e >= 2:
                    dve.wait_ge(y_step, e - 1)
                v.tensor_tensor_reduce(out=junk[e % 2], in0=w2_sb[:, e], in1=P[e % 4][:, :], scale=1.0, scalar=0.0,
                                       op0=ALU.mult, op1=ALU.add, accum_out=y[:, e:e + 1]).then_inc(y_step, 1)
            dve.wait_ge(y_step, E)
            v.tensor_tensor(yrep[:], y.unsqueeze(1).to_broadcast([128, HB, E]),
                            small[:, 6].unsqueeze(1).to_broadcast([128, HB, E]), ALU.mult).then_inc(y_step, 1)
            dve.wait_ge(y_transposed, 1)
            for b in range(HB):
                dve.wait_ge(yh_ready, b + 1)
                a = v.scalar_tensor_tensor(out=yl[:, b], in0=P[5][:, 0:128], scalar=bmask[:, b:b + 1],
                                           in1=yh[:, b].bitcast(FP32), op0=ALU.mult, op1=ALU.subtract)
                if b % 4 == 3:
                    a.then_inc(yl_ready, 1)
            for n in range(2 * NHB):
                dve.wait_ge(mix_mm, n + 1)
                hv = H[0:T, 4 * n:4 * (n + 1)].rearrange("p b c -> p (b c)")
                v.tensor_tensor(hv, P[n % 4][0:T, :], hv, ALU.add).then_inc(mixed, 1)


_INS = ["x", "L0_tok_kernel", "L0_attn_A", "L0_attn_B", "L0_attn_h0", "L0_ffn_gate_weight", "L0_ffn_w1", "L0_ffn_w2"]


def kernel(**inputs):
    import numpy as _np
    import concourse.bacc as _bacc
    from concourse import mybir as _mybir
    from concourse.bass_utils import run_bass_kernel_spmd as _run

    nc = _bacc.Bacc("TRN2", target_bir_lowering=False, num_devices=1)
    arrays, args = {}, []
    for name in _INS:
        arrays[f"in_{name}"] = _np.ascontiguousarray(inputs[name])
    for name, a in tables().items():
        arrays[f"const_{name}"] = a
    for name, a in arrays.items():
        args.append(nc.dram_tensor(name, a.shape, _mybir.dt.from_np(a.dtype), kind="ExternalInput").ap())
    args.append(nc.dram_tensor("out", (B, T, D), FP32, kind="ExternalOutput").ap())
    args.append(nc.dram_tensor("kpad", (D, KROW), FP32, kind="Internal").ap())
    args.append(nc.dram_tensor("table", ((B + 1) * TROW, D), FP32, kind="Internal").ap())
    build(nc, *args)
    return _run(nc, [arrays], core_ids=[0]).results[0]["out"]
```
